# Optimizing a Trainium2 kernel written in Bass

```python
import numpy as np
import jax
import jax.numpy as jnp

def _softmax(x, axis=-1):
    return jax.nn.softmax(x, axis=axis)
def _gelu(x):
    return jax.nn.gelu(x, approximate=True)
def _silu(x):
    return jax.nn.silu(x)
def _sigmoid(x):
    return jax.nn.sigmoid(x)
def _layernorm(x, axis=-1, eps=1e-5):
    m = jnp.mean(x, axis=axis, keepdims=True)
    v = jnp.var(x, axis=axis, keepdims=True)
    return (x - m) / jnp.sqrt(v + eps)
def _scatter_add(tgt, idx, src, axis=0):
    return tgt.at[idx].add(src)
def _segment_sum(src, seg, n):
    return jax.ops.segment_sum(src, seg, n)

kernel_name = 'mk_adj_resnorm_d2_adj_64_5a3f1b'

def setup_inputs(seed: int = 0):
    np.random.seed(seed)
    _w = jnp.asarray
    def _rec_inputs():
        import jax
        import jax.numpy as jnp
        _gk = jax.random.key(seed)
        x = -0.0001071 + 1.001 * jax.random.normal(jax.random.fold_in(_gk, 1), (8, 3000, 64), jnp.float32)
        _a = jax.random.bernoulli(jax.random.fold_in(_gk, 2), 0.00533333, (8, 3000, 3000))
        _af = _a.astype(jnp.float32)
        adj = _af
        return x, adj
    x, adj = _rec_inputs()
    def _L0_gnn_setup():
        import jax, jax.numpy as jnp
        import numpy as np
        B, N, F = (2, 3000, 64)
        H, OUT, ATT = (4, 16, 16)
        DENSITY = 0.01
        key = jax.random.key(seed)
        ks = jax.random.split(key, 6)
        h = jax.random.normal(ks[0], (B, N, F), dtype=jnp.float32)
        a = (jax.random.uniform(ks[1], (B, N, N)) < DENSITY).astype(jnp.float32)
        glorot = lambda k, shape: jax.random.uniform(k, shape, jnp.float32, -1.0, 1.0) * jnp.sqrt(6.0 / (shape[-2] + shape[-1]))
        kernel = glorot(ks[2], (H, F, OUT))
        attention_kernel = glorot(ks[3], (H, F, ATT))
        attention_kernel_2 = glorot(ks[4], (H, F, ATT))
        bias = jax.random.normal(ks[5], (1, 1, H, OUT), dtype=jnp.float32) * 0.01
        return {'h': h, 'a': a, 'kernel': kernel, 'attention_kernel': attention_kernel, 'attention_kernel_2': attention_kernel_2, 'bias': bias}
    _L0_gnn_all = _L0_gnn_setup()
    _L0_gnn_in = {k: v for k, v in _L0_gnn_all.items() if k in ('kernel', 'attention_kernel', 'attention_kernel_2', 'bias', )}
    del _L0_gnn_all

    def _L1_gnn_setup():
        import jax, jax.numpy as jnp
        import numpy as np
        B, N, C = (8, 2048, 64)
        N_LAYERS = 3

        def _graph_conv(X, A, Wm, Ws, b):
            M = jnp.einsum('bnc,oc->bno', X, Wm)
            M = jnp.matmul(A, M)
            return M + jnp.einsum('bnc,oc->bno', X, Ws) + b
        key = jax.random.key(seed)
        ks = jax.random.split(key, 2 + 3 * N_LAYERS)
        X = jax.random.normal(ks[0], (B, N, C), dtype=jnp.float32)
        A = jax.random.uniform(ks[1], (B, N, N), dtype=jnp.float32)
        inp = {'X': X, 'A': A}
        bound_w = np.sqrt(3.0) * (np.sqrt(2.0 / (1.0 + 5.0)) / np.sqrt(C))
        bound_b = 1.0 / np.sqrt(C)
        for l in range(N_LAYERS):
            inp[f'Wm{l}'] = jax.random.uniform(ks[2 + 3 * l], (C, C), minval=-bound_w, maxval=bound_w, dtype=jnp.float32)
            inp[f'Ws{l}'] = jax.random.uniform(ks[3 + 3 * l], (C, C), minval=-bound_w, maxval=bound_w, dtype=jnp.float32)
            inp[f'b{l}'] = jax.random.uniform(ks[4 + 3 * l], (C,), minval=-bound_b, maxval=bound_b, dtype=jnp.float32)
        return inp
    _L1_gnn_all = _L1_gnn_setup()
    _L1_gnn_in = {k: v for k, v in _L1_gnn_all.items() if k in ('Wm0', 'Ws0', 'b0', 'Wm1', 'Ws1', 'b1', 'Wm2', 'Ws2', 'b2', )}
    del _L1_gnn_all

    return {
        "x": x,
        "adj": adj,
        "L0_gnn_kernel": _L0_gnn_in["kernel"],
        "L0_gnn_attention_kernel": _L0_gnn_in["attention_kernel"],
        "L0_gnn_attention_kernel_2": _L0_gnn_in["attention_kernel_2"],
        "L0_gnn_bias": _L0_gnn_in["bias"],
        "L1_gnn_Wm0": _L1_gnn_in["Wm0"],
        "L1_gnn_Ws0": _L1_gnn_in["Ws0"],
        "L1_gnn_b0": _L1_gnn_in["b0"],
        "L1_gnn_Wm1": _L1_gnn_in["Wm1"],
        "L1_gnn_Ws1": _L1_gnn_in["Ws1"],
        "L1_gnn_b1": _L1_gnn_in["b1"],
        "L1_gnn_Wm2": _L1_gnn_in["Wm2"],
        "L1_gnn_Ws2": _L1_gnn_in["Ws2"],
        "L1_gnn_b2": _L1_gnn_in["b2"],
    }

def reference(x, adj, L0_gnn_kernel, L0_gnn_attention_kernel, L0_gnn_attention_kernel_2, L0_gnn_bias, L1_gnn_Wm0, L1_gnn_Ws0, L1_gnn_b0, L1_gnn_Wm1, L1_gnn_Ws1, L1_gnn_b1, L1_gnn_Wm2, L1_gnn_Ws2, L1_gnn_b2):
    import jax
    import jax.numpy as jnp
    def _L0_gnn_ref(h, a, kernel, attention_kernel, attention_kernel_2, bias):
        import jax, jax.numpy as jnp
        import numpy as np
        B, N, F = (2, 3000, 64)
        H, OUT, ATT = (4, 16, 16)
        DENSITY = 0.01
        feats = jnp.einsum('bnf,hfo->bhno', h, kernel)
        f_self = jnp.einsum('bnf,hfd->hbnd', h, attention_kernel)
        f_other = jnp.einsum('bnf,hfd->hbdn', h, attention_kernel_2)
        a_h = a[None]
        scores = jnp.einsum('hbnd,hbdm->hbnm', f_self, f_other)
        masked = a_h * scores
        masked = jnp.where(masked >= 0, masked, 0.2 * masked)
        masked = masked / jnp.sqrt(jnp.float32(ATT))
        masked = masked + jnp.where(a_h == 0, jnp.float32(-1000000000.0), jnp.float32(0.0))
        attn = jax.nn.softmax(masked, axis=-1)
        attn = attn * jnp.where(a_h == 0, jnp.float32(0.0), jnp.float32(1.0))
        attn = jnp.transpose(attn, (1, 0, 2, 3))
        node_features = jnp.einsum('bhnm,bhmo->bhno', attn, feats)
        node_features = node_features + jnp.transpose(bias, (0, 2, 1, 3))
        node_features = jax.nn.relu(node_features)
        node_features = jnp.transpose(node_features, (0, 2, 1, 3))
        return node_features.reshape(-1, N, H * OUT)

    def _L1_gnn_ref(X, A, Wm0, Ws0, b0, Wm1, Ws1, b1, Wm2, Ws2, b2):
        import jax, jax.numpy as jnp
        import numpy as np
        B, N, C = (8, 2048, 64)
        N_LAYERS = 3

        def _graph_conv(X, A, Wm, Ws, b):
            M = jnp.einsum('bnc,oc->bno', X, Wm)
            M = jnp.matmul(A, M)
            return M + jnp.einsum('bnc,oc->bno', X, Ws) + b
        H = jax.nn.relu(_graph_conv(X, A, Wm0, Ws0, b0))
        H = jax.nn.relu(_graph_conv(H, A, Wm1, Ws1, b1))
        H = _graph_conv(H, A, Wm2, Ws2, b2)
        return H

    x = _layernorm(x + _L0_gnn_ref(x, adj, L0_gnn_kernel, L0_gnn_attention_kernel, L0_gnn_attention_kernel_2, L0_gnn_bias), axis=-1)
    x = _layernorm(x + _L1_gnn_ref(x, adj, L1_gnn_Wm0, L1_gnn_Ws0, L1_gnn_b0, L1_gnn_Wm1, L1_gnn_Ws1, L1_gnn_b1, L1_gnn_Wm2, L1_gnn_Ws2, L1_gnn_b2), axis=-1)
    return x


_drawn_inputs = setup_inputs


def setup_inputs(seed=0):
    import zlib

    import numpy as np

    out = dict(_drawn_inputs(seed))
    spreads = {}
    factors = {'L0_gnn_bias': 2.809, 'L1_gnn_b1': 7.972, 'L1_gnn_b2': 43.571}
    for name, (base, spread) in spreads.items():
        noise = np.random.default_rng([zlib.crc32(name.encode()), seed]).standard_normal(out[name].shape)
        drawn = base * np.exp(spread * noise) if base else spread * noise
        out[name] = jnp.asarray(drawn.astype(out[name].dtype))
    for name, factor in factors.items():
        out[name] = (out[name] * factor).astype(out[name].dtype)
    return out
```

```python
from contextlib import ExitStack

import concourse.bass as bass
from concourse import mybir

F32 = mybir.dt.float32
BF16 = mybir.dt.bfloat16
FP8 = mybir.dt.float8e4
U8 = mybir.dt.uint8
ALU = mybir.AluOpType
ACT = mybir.ActivationFunctionType
AX = mybir.AxisListType

B, N, F = 8, 3000, 64
H, D = 4, 16
HD = H * D
P = 125
T = N // P
CT = 4
C = CT * P
NC = N // C
PIECE = 2 * C
NJ = N // PIECE
BPP = PIECE // P
LAYERS = 3
PAIRS = H // 2
KS = 6 * D
KX = KS + 2
V = D + 1
UNITS = CT * NJ * H
assert UNITS == T * PAIRS
PIECES = CT * NJ
LAG = 3
BIG = 2.0 ** 35
ONE8 = 56.0
EPS = 1e-5
NEG = -3.0e38
PART_S = (0, 0, 1, 1, 0, 2)
PART_O = (0, 1, 0, 1, 2, 0)


def region_plan():
    plan = [(4 * p + 1, "mask", p) for p in range(PIECES)]
    plan += [(12 * t + 14, "shift", t) for t in range(CT)]
    return sorted(plan)


PLAN = region_plan()
MISC_A, MISC_B = len(PLAN), 1
MISC_GRAPH = NC * (MISC_A + MISC_B)
TURN_OF = {(kind, i): n for n, (_, kind, i) in enumerate(PLAN)}


def build(nc, x, adj, kernel, att1, att2, bias, wm, ws, bb, out):
    scratch = nc.dram_tensor("scratch", (3, 2 * HD, N), BF16, kind="Internal").ap()

    with ExitStack() as ctx:
        def sb(name, shape, dt):
            return ctx.enter_context(nc.sbuf_tensor(name, shape, dt))

        def psum(name, shape, dt):
            return ctx.enter_context(nc.psum_tensor(name, shape, dt))

        def sem(name):
            return ctx.enter_context(nc.semaphore(name))

        AT = sb("AT", [P, T, N], U8)
        MT = sb("MT", [P, 2, T, C], BF16)
        FO = sb("FO", [KX, H, N], BF16)
        FS = sb("FS", [KS, 3, H, C], BF16)
        FQ = sb("FQ", [KX, 2, H, C], BF16)
        A32 = sb("A32", [P, 2, PIECE], F32)
        M16 = sb("M16", [P, 3, PIECE], BF16)
        E = sb("E", [128, 4, PIECE], F32)
        VA = sb("VA", [P, T, H, V], F32)
        OT = sb("OT", [128, C], F32)
        ON = sb("ON", [P, CT, H, V], F32)
        H0 = sb("H0", [P, T, HD], F32)
        ident = sb("ident", [128, 128], F32)
        ident16 = sb("ident16", [128, 128], BF16)
        cm = sb("cm", [P, H, NJ], F32)
        mx = sb("mx", [P, H], F32)
        sh = sb("sh", [P, H], F32)
        sh2 = sb("sh2", [P, H], F32)
        shift = sb("shift", [P, H, 2], BF16)
        den = sb("den", [P, CT, H], F32)
        rden = sb("rden", [P, CT, H], F32)
        wqk = sb("wqk", [F, 2 * HD], F32)
        wv = sb("wv", [F, HD], F32)
        biasb = sb("biasb", [P, HD], F32)
        HT = sb("HT", [F + 1, N], F32)
        W3 = sb("W3", [F + 1, LAYERS, 2 * F], F32)
        floor = sb("floor", [P, LAYERS], F32)
        mean = sb("mean", [P, T], F32)
        var = sb("var", [P, T], F32)
        std = sb("std", [P, T], F32)
        rstd = sb("rstd", [P, T], F32)

        work = MT[:, :, :, :].rearrange("p a t c -> p (a t c)").bitcast(F32)
        TF = T * F
        X = work[:, 0:TF].rearrange("p (t f) -> p t f", f=F)
        HC = work[:, TF:2 * TF].rearrange("p (t f) -> p t f", f=F)
        SELF = work[:, 2 * TF:3 * TF].rearrange("p (t f) -> p t f", f=F)
        TMP = work[:, 3 * TF:4 * TF].rearrange("p (t f) -> p t f", f=F)
        M3 = work[:, 4 * TF:4 * TF + T * 3 * F // 2].bitcast(BF16).rearrange("p (t c) -> p t c", c=3 * F)
        assert 4 * TF + T * 3 * F // 2 <= T * C
        free = E[:, :, :].rearrange("p s c -> p (s c)")
        xin = free[0:P, 0:2 * CT * F].rearrange("p (s t f) -> p s t f", s=2, f=F)
        at = 2 * CT * F
        xT = free[0:F, at:at + 2 * C].rearrange("p (s c) -> p s c", s=2)
        at += 2 * C
        rest = free[:, at:at + C]
        at += C
        parts = free[:, at:at + 3 * C].bitcast(BF16).rearrange("p (s a c) -> p s a c", s=2, a=3)
        assert at + 3 * C <= 4 * PIECE and 2 * HD == 128

        pA = psum("pA", [128, 2, 512], F32)
        pB = psum("pB", [128, 2, 2, 512], F32)
        pO = psum("pO", [128, 512], F32)
        misc = psum("misc", [128, 512], F32)
        misc16 = misc[:, :].bitcast(BF16).rearrange("p (b c) -> p b c", c=128)
        pAcc = pB[:, :, :, :].rearrange("p a b c -> p (a b) c")

        w_loaded = sem("w_loaded")
        consts = sem("consts")
        ident_step = sem("ident_step")
        w_turned = sem("w_turned")
        w_placed = sem("w_placed")
        x_in = [sem("x_in0"), sem("x_in1")]
        x_turned = sem("x_turned")
        x_sb = sem("x_sb")
        proj_full = sem("proj_full")
        val_full = sem("val_full")
        high_done = sem("high_done")
        val_done = sem("val_done")
        rest_done = sem("rest_done")
        mid_done = sem("mid_done")
        parts_done = sem("parts_done")
        scr_out = [sem("scr_out0"), sem("scr_out1")]
        fo_in = sem("fo_in")
        fs_in = sem("fs_in")
        a_in = [sem("a_in0"), sem("a_in1")]
        m16_ready = sem("m16_ready")
        fq_ready = sem("fq_ready")
        sn_full = sem("sn_full")
        max_done = sem("max_done")
        stat = sem("stat")
        shift_done = sem("shift_done")
        misc_full = sem("misc_full")
        misc_done = sem("misc_done")
        at_done = sem("at_done")
        sm_full = sem("sm_full")
        relu_done = sem("relu_done")
        sx_full = sem("sx_full")
        exp_done = sem("exp_done")
        pv_done = sem("pv_done")
        ot_done = sem("ot_done")
        fin = sem("fin")
        x_res = sem("x_res")
        ln = sem("ln")
        std_done = sem("std_done")
        x1_done = sem("x1_done")
        hc_ready = sem("hc_ready")
        ht_full = sem("ht_full")
        ht_done = sem("ht_done")
        wx_full = sem("wx_full")
        self_done = sem("self_done")
        m3_step = sem("m3_step")
        m3_done = sem("m3_done")
        acc_full = sem("acc_full")
        acc_done = sem("acc_done")
        add_done = sem("add_done")
        y_done = sem("y_done")
        y_out = sem("y_out")
        passed = sem("passed")

        x_v = x.rearrange("b (t p) f -> b p t f", p=P)
        out_v = out.rearrange("b (t p) f -> b p t f", p=P)
        adj_v = adj.rearrange("b (t p) (j c) -> b t j p c", p=P, c=PIECE)
        scr_v = scratch.rearrange("a p n -> p a n")
        id_p = ident[0:P, 0:P]
        id16 = ident16[0:P, 0:P]

        def banks(ap):
            return ap.rearrange("p (a c) -> p a c", a=2)

        def bank_a(both, u):
            return (pA[:, :, :], pB[:, 0, :, :], pB[:, 1, :, :])[0 if both else u % 3]

        def bank_b(both, u):
            return (pB[:, 0, :, :], pB[:, 1, :, :], pA[:, :, :])[u % 2 if both else u % 3]

        def chunks(b, k):
            return b * NC + k

        def turns(b, k):
            if isinstance(k, int) and k == 0:
                return b * MISC_GRAPH
            return b * MISC_GRAPH + k * (MISC_A + MISC_B) - MISC_B

        N_CONST = 7

        def apart(eng):
            eng.sem_inc(passed, 1)

        block = ctx.enter_context(nc.Block())

        @block.sync
        def _(sp):
            for dst, src in ((wqk[:, 0:HD], att1), (wqk[:, HD:2 * HD], att2), (wv[:, :], kernel)):
                sp.dma_start(dst.rearrange("f (h d) -> f h d", h=H), src.rearrange("h f d -> f h d")
                             ).then_inc(w_loaded, 16)
            sp.dma_start(biasb[:, :], bias.rearrange("a b h d -> (a b h d)").partition_broadcast(P)
                         ).then_inc(w_loaded, 16)
            for l in range(LAYERS):
                sp.dma_start(SELF[0:F, l, :], ws[l]).then_inc(w_loaded, 16)
                sp.dma_start(TMP[0:F, l, :], wm[l]).then_inc(w_loaded, 16)
            sp.wait_ge(consts, N_CONST)
            for l in range(LAYERS):
                sp.dma_start(W3[F:F + 1, l, 0:F], bb[l].unsqueeze(0)).then_inc(w_loaded, 16)

            def load_x(b, c):
                if c >= 2:
                    sp.wait_ge(x_turned, chunks(b, c) - 1)
                    apart(sp)
                sp.dma_start(xin[:, c % 2, :, :], x_v[b, :, CT * c:CT * c + CT, :]
                             ).then_inc(x_in[c % 2], 16)

            def load_queries(k, slot):
                for g in range(6):
                    sp.dma_start(FS[D * g:D * g + D, slot, :, :],
                                 scratch[PART_S[g], 0:HD, bass.ds(k * C, C)].rearrange(
                                     "(h d) n -> d h n", h=H)).then_inc(fs_in, 16)

            def load_rows(b, k):
                for p in range(PIECES):
                    sp.wait_ge(m16_ready, chunks(b, k) * PIECES + p + 1)
                    apart(sp)
                    sp.dma_start(A32[:, p % 2, :], adj_v[b, k * CT + p // NJ, p % NJ]
                                 ).then_inc(a_in[p % 2], 16)

            with sp.Fori(0, B) as b:
                sp.wait_ge(y_done, b + 1)
                apart(sp)
                load_x(b, 0)
                load_x(b, 1)
                for c in range(NC):
                    sp.wait_ge(parts_done, chunks(b, c) + 1)
                    apart(sp)
                    sp.dma_start(scr_v[:, :, C * c:C * c + C], parts[:, c % 2, :, :]
                                 ).then_inc(scr_out[c % 2], 16)
                    if c + 2 < NC:
                        load_x(b, c + 2)
                for s in scr_out:
                    sp.wait_ge(s, (b + 1) * (16 * NC // 2))
                apart(sp)
                for g in range(6):
                    sp.dma_start(FO[D * g:D * g + D, :, :],
                                 scratch[PART_O[g], HD:2 * HD, :].rearrange("(h d) n -> d h n", h=H)
                                 ).then_inc(fo_in, 16)
                load_queries(0, 0)
                load_rows(b, 0)
                load_queries(1, 1)
                with sp.Fori(1, NC - 1) as k:
                    load_rows(b, k)
                    load_queries(k + 1, (k + 1) % 3)
                load_rows(b, NC - 1)
                sp.wait_ge(relu_done, (b + 1) * (NC * UNITS))
                apart(sp)
                sp.wait_ge(at_done, (b + 1) * T)
                apart(sp)
                sp.dma_start(X, x_v[b]).then_inc(x_res, 16)
                sp.wait_ge(y_done, b + 2)
                apart(sp)
                sp.dma_start(out_v[b], HC).then_inc(y_out, 16)
                sp.wait_ge(y_out, (b + 1) * 16)
                apart(sp)

        @block.tensor
        def _(pe):
            mm = nc.tensor.matmul

            pe.wait_ge(ident_step, 3)
            pe.wait_ge(w_loaded, 16 * (4 + 3 * LAYERS))
            for l in range(LAYERS):
                for o, w in ((0, SELF), (F, TMP)):
                    last = nc.tensor.transpose(pA[0:F, 0, 2 * F * l + o:2 * F * l + o + F], w[0:F, l, :],
                                               ident[0:F, 0:F])
            last.then_inc(w_turned, 1)
            pe.wait_ge(w_placed, 1)

            def prologue(b):
                for c in range(NC + 1):
                    if c < NC:
                        pe.wait_ge(x_in[c % 2], (b * (NC // 2) + c // 2 + 1) * 16)
                        if c >= 2:
                            pe.wait_ge(x_sb, chunks(b, c) - 1)
                        apart(pe)
                        for t in range(CT):
                            last = nc.tensor.transpose(pA[0:F, c % 2, P * t:P * t + P], xin[:, c % 2, t, :],
                                                       id_p)
                        last.then_inc(x_turned, 1)
                    if c >= 1:
                        d = c - 1
                        pe.wait_ge(x_sb, chunks(b, d) + 1)
                        if d >= 2:
                            pe.wait_ge(rest_done, chunks(b, d) - 1)
                            pe.wait_ge(val_done, chunks(b, d) - 1)
                        mm(pB[:, 0, d % 2, 0:C], wqk[:, :], xT[:, d % 2, :], start=True, stop=True
                           ).then_inc(proj_full, 1)
                        for t in range(CT):
                            last = mm(pB[0:P, 1, d % 2, F * t:F * t + F], xT[:, d % 2, P * t:P * t + P],
                                      wv[:, :], start=True, stop=True)
                        last.then_inc(val_full, 1)

            def scores_a(b, k, u, both):
                t, j, h = u // (NJ * H), u // H % NJ, u % H
                if u == 0:
                    pe.wait_ge(fs_in, (chunks(b, k) + 1) * 96)
                if both:
                    pe.wait_ge(max_done, chunks(b, k) * UNITS + u + 1)
                elif u >= 3:
                    pe.wait_ge(max_done, chunks(b, k) * UNITS + u - 1)
                for a in range(2):
                    last = mm(bank_a(both, u)[0:P, a, 0:C], FS[:, k % 3, h, P * t:P * t + P],
                              FO[0:KS, h, PIECE * j + C * a:PIECE * j + C * a + C], start=True, stop=True)
                last.then_inc(sn_full, 1)

            def turn(b, k, kind, i):
                n = turns(b, k) + TURN_OF[kind, i]
                pe.wait_ge(misc_done, n + 1)
                if kind == "mask":
                    pe.wait_ge(m16_ready, chunks(b, k) * PIECES + i + 3)
                    for s in range(BPP):
                        last = nc.tensor.transpose(misc16[0:P, s, 0:P], M16[:, i % 3, P * s:P * s + P], id16)
                else:
                    pe.wait_ge(shift_done, chunks(b, k) * CT + i + 1)
                    for h in range(H):
                        last = nc.tensor.transpose(misc16[KS:KX, h, 0:P], shift[:, h, :], id16)
                last.then_inc(misc_full, 1)

            def scores_b(b, k, u, both):
                i, pair = u // PAIRS, u % PAIRS
                pe.wait_ge(exp_done, chunks(b, k) * UNITS + u + (1 if both else 0))
                for a in range(2):
                    h = 2 * pair + a
                    last = mm(bank_b(both, u)[0:P, a, 0:C], FO[0:KS, h, P * i:P * i + P], FS[:, k % 3, h, :],
                              start=True, stop=True)
                last.then_inc(sm_full, 1)

            def exponent_b(b, k, u, both):
                i, pair = u // PAIRS, u % PAIRS
                if u == 0:
                    pe.wait_ge(fq_ready, chunks(b, k) + 1)
                    pe.wait_ge(misc_done, turns(b, k + 1) + 1)
                pe.wait_ge(relu_done, chunks(b, k) * UNITS + u + 1)
                for a in range(2):
                    h = 2 * pair + a
                    last = mm(bank_b(both, u)[0:P, a, 0:C], FO[0:KX, h, P * i:P * i + P], FQ[:, k % 2, h, :],
                              start=False, stop=True, skip_group_check=True)
                last.then_inc(sx_full, 1)

            def values_b(b, k, i):
                pe.wait_ge(exp_done, chunks(b, k) * UNITS + 2 * i + 4)
                for h in range(H):
                    last = mm(pO[32 * h:32 * h + V, 0:C], VA[:, i, h, :],
                              E[0:P, (2 * i + h // 2) % 4, C * (h % 2):C * (h % 2) + C],
                              start=(i == 0), stop=(i == T - 1))
                last.then_inc(pv_done, 1)

            def region(b, k, a, bb_):
                both = a and bb_
                lag = LAG if both else 0
                ahead = 1 if both else 2
                plan = list(PLAN) if a else []
                if bb_:
                    for u in range(ahead):
                        scores_b(b, k - 1, u, both)
                for s in range(UNITS + 4):
                    if bb_ and 1 <= s <= UNITS:
                        exponent_b(b, k - 1, s - 1, both)
                    if bb_ and s >= 4 and s % 2 == 0:
                        values_b(b, k - 1, (s - 4) // 2)
                    u = s + 1 - lag
                    if a and 0 <= u < UNITS + lag:
                        if s == 0 and lag == 0:
                            scores_a(b, k, 0, both)
                        if u < UNITS:
                            scores_a(b, k, u, both)
                        while plan and plan[0][0] <= u:
                            turn(b, k, *plan.pop(0)[1:])
                    if bb_ and s + ahead < UNITS:
                        scores_b(b, k - 1, s + ahead, both)
                for _, kind, i in plan:
                    turn(b, k, kind, i)
                if bb_:
                    pe.wait_ge(ot_done, (chunks(b, k - 1) + 1) * H)
                    n = turns(b, k) + (MISC_A if a else 0)
                    pe.wait_ge(misc_done, n + 1)
                    apart(pe)
                    for t in range(CT):
                        last = nc.tensor.transpose(misc[0:P, 128 * t:128 * t + 128], OT[:, P * t:P * t + P],
                                                   ident[:, :])
                    last.then_inc(misc_full, 1)

            wx = (pO, misc)

            def layer(b, l):
                n = b * LAYERS + l
                pe.wait_ge(hc_ready, b * (LAYERS + 1) + l + 1)
                for g in range(NC + 1):
                    if g < NC:
                        if g >= 2:
                            pe.wait_ge(ht_done, n * NC + g - 1)
                        apart(pe)
                        for t in range(CT):
                            last = nc.tensor.transpose(pA[0:F, g % 2, P * t:P * t + P], HC[:, CT * g + t, :],
                                                       id_p)
                        last.then_inc(ht_full, 1)
                    if g >= 1:
                        d = g - 1
                        pe.wait_ge(ht_done, n * NC + d + 1)
                        if d >= 2:
                            pe.wait_ge(m3_done, n * NC + d - 1)
                            pe.wait_ge(self_done, n * NC + d - 1)
                        for t in range(CT):
                            q = C * d + P * t
                            last = mm(wx[d % 2][0:P, 2 * F * t:2 * F * t + 2 * F], HT[:, q:q + P],
                                      W3[:, l, :], start=True, stop=True)
                        last.then_inc(wx_full, 1)
                pe.wait_ge(m3_done, (n + 1) * NC)
                apart(pe)
                for t in range(T):
                    if t % 2 == 0 and t >= 8:
                        pe.wait_ge(acc_done, n * (T // 2) + t // 2 - 3)
                        apart(pe)
                    for i in range(T):
                        last = mm(pAcc[0:P, t // 2 % 4, 3 * F * (t % 2):3 * F * (t % 2) + 3 * F],
                                  AT[:, i, P * t:P * t + P].bitcast(FP8), M3[:, i, :],
                                  start=(i == 0), stop=(i == T - 1))
                    if t % 2:
                        last.then_inc(acc_full, 1)

            with pe.Fori(0, B) as b:
                prologue(b)
                pe.wait_ge(rest_done, chunks(b, NC))
                pe.wait_ge(val_done, chunks(b, NC))
                pe.wait_ge(fo_in, (b + 1) * 96)
                region(b, 0, True, False)
                with pe.Fori(1, NC) as k:
                    region(b, k, True, True)
                region(b, NC, False, True)
                with pe.Fori(0, LAYERS) as l:
                    layer(b, l)

        @block.vector
        def _(dve):
            v = nc.vector
            v.memset(FO[KS:KX, :, :], 1.0).then_inc(consts, 1)
            v.memset(VA[:, :, :, :], 1.0).then_inc(consts, 1)
            v.memset(OT[:, :], 0.0).then_inc(consts, 1)
            v.memset(W3[:, :, :], 0.0).then_inc(consts, 1)
            v.memset(HT[F:F + 1, :], 1.0).then_inc(consts, 1)
            v.memset(floor[:, 0:LAYERS - 1], 0.0).then_inc(consts, 1)
            v.memset(floor[:, LAYERS - 1:LAYERS], NEG).then_inc(consts, 1)
            dve.sem_inc(max_done, 1)
            dve.sem_inc(y_done, 1)
            dve.sem_inc(exp_done, 2)
            dve.sem_inc(misc_done, 1)
            dve.sem_inc(m16_ready, 2)
            dve.wait_ge(consts, N_CONST)

            def prologue(b):
                for c in range(NC):
                    n = chunks(b, c) + 1
                    dve.wait_ge(high_done, n)
                    if c >= 1:
                        dve.wait_ge(parts_done, n - 1)
                    v.tensor_tensor(rest, pB[:, 0, c % 2, 0:C], parts[:, c % 2, 0, :], ALU.subtract
                                    ).then_inc(rest_done, 1)
                    dve.wait_ge(rest_done, n)
                    v.tensor_copy(parts[:, c % 2, 1, :], rest).then_inc(mid_done, 1)
                    dve.wait_ge(mid_done, n)
                    v.tensor_tensor(parts[:, c % 2, 2, :], rest, parts[:, c % 2, 1, :], ALU.subtract
                                    ).then_inc(parts_done, 1)

            def maximum_a(b, k, u, both):
                p, h = u // H, u % H
                if h == 0:
                    dve.wait_ge(m16_ready, chunks(b, k) * PIECES + p + 3)
                dve.wait_ge(sn_full, chunks(b, k) * UNITS + u + 1)
                apart(dve)
                pu = bank_a(both, u)[0:P, :, 0:C]
                v.tensor_tensor_reduce(pu, pu, banks(M16[:, p % 3, :]), 1.0, NEG,
                                       ALU.add, ALU.max, cm[:, h, p % NJ:p % NJ + 1]).then_inc(max_done, 1)

            def shifts_a(b, k, t):
                n = (chunks(b, k) * CT + t) * 4
                dve.wait_ge(max_done, chunks(b, k) * UNITS + (t + 1) * NJ * H + 1)
                v.tensor_reduce(mx[:, :], cm[:, :, :], AX.X, ALU.max).then_inc(stat, 1)
                dve.wait_ge(stat, n + 1)
                v.tensor_scalar(sh2[:, :], mx[:, :], -1.25, None, ALU.mult).then_inc(stat, 1)
                dve.wait_ge(stat, n + 2)
                v.scalar_tensor_tensor(out=sh[:, :], in0=mx[:, :], scalar=-0.25, op0=ALU.mult,
                                       in1=sh2[:, :], op1=ALU.min).then_inc(stat, 1)
                dve.wait_ge(stat, n + 3)
                v.tensor_copy(shift[:, :, 0], sh[:, :]).then_inc(stat, 1)
                dve.wait_ge(stat, n + 4)
                v.tensor_tensor(shift[:, :, 1], sh[:, :], shift[:, :, 0], ALU.subtract
                                ).then_inc(shift_done, 1)

            def relu_b(b, k, u, both):
                if u == 0:
                    dve.wait_ge(misc_done, turns(b, k + 1) + 1)
                dve.wait_ge(sm_full, chunks(b, k) * UNITS + u + 1)
                i = u // PAIRS
                pu = bank_b(both, u)[0:P, :, 0:C]
                v.scalar_tensor_tensor(out=pu, in0=pu, scalar=0.0,
                                       op0=ALU.max, in1=MT[:, k % 2, i, :].unsqueeze(1).broadcast_to([P, 2, C]),
                                       op1=ALU.add).then_inc(relu_done, 1)

            def finish_b(b, k, n):
                f = chunks(b, k) * 5
                h0 = H0[:, bass.ds(k * CT, CT), :]
                h04 = h0.rearrange("p t (h d) -> p t h d", h=H)
                dve.wait_ge(misc_done, n + 2)
                v.tensor_scalar(den[:, :, :], ON[:, :, :, D], 1e-30, None, ALU.max).then_inc(fin, 1)
                dve.wait_ge(fin, f + 1)
                v.reciprocal(rden[:, :, :], den[:, :, :]).then_inc(fin, 1)
                dve.wait_ge(fin, f + 2)
                v.tensor_tensor(h04, ON[:, :, :, 0:D], rden[:, :, :].unsqueeze(3).broadcast_to([P, CT, H, D]),
                                ALU.mult).then_inc(fin, 1)
                dve.wait_ge(fin, f + 3)
                v.tensor_tensor(h0, h0, biasb[:, :].unsqueeze(1).broadcast_to([P, CT, HD]), ALU.add
                                ).then_inc(fin, 1)
                dve.wait_ge(fin, f + 4)
                v.tensor_scalar(h0, h0, 0.0, None, ALU.max).then_inc(fin, 1)

            def region(b, k, a, bb_):
                lag = LAG if a and bb_ else 0
                for s in range(UNITS + lag):
                    if a and 0 <= s - lag < UNITS:
                        maximum_a(b, k, s - lag, bb_)
                        if (s - lag + 1) % (NJ * H) == 0:
                            shifts_a(b, k, (s - lag) // (NJ * H))
                    if bb_ and s < UNITS:
                        relu_b(b, k - 1, s, a)
                if bb_:
                    finish_b(b, k - 1, turns(b, k) + (MISC_A if a else 0))

            def layernorm(n, m, first_in, dst, done):
                def bc(s):
                    return s[:, :].unsqueeze(2).broadcast_to([P, T, F])
                v.tensor_tensor(X, X, first_in, ALU.add).then_inc(ln, 1)
                dve.wait_ge(ln, n + 1)
                v.tensor_reduce(mean[:, :], X, AX.X, ALU.add).then_inc(ln, 1)
                dve.wait_ge(ln, n + 2)
                v.tensor_scalar(mean[:, :], mean[:, :], 1.0 / F, None, ALU.mult).then_inc(ln, 1)
                dve.wait_ge(ln, n + 3)
                v.tensor_tensor(X, X, bc(mean), ALU.subtract).then_inc(ln, 1)
                dve.wait_ge(ln, n + 4)
                v.tensor_tensor(TMP, X, X, ALU.mult).then_inc(ln, 1)
                dve.wait_ge(ln, n + 5)
                v.tensor_reduce(var[:, :], TMP, AX.X, ALU.add).then_inc(ln, 1)
                dve.wait_ge(ln, n + 6)
                v.tensor_scalar(var[:, :], var[:, :], 1.0 / F, EPS, ALU.mult, ALU.add).then_inc(ln, 1)
                dve.wait_ge(std_done, m)
                v.reciprocal(rstd[:, :], std[:, :]).then_inc(ln, 1)
                dve.wait_ge(ln, n + 8)
                v.tensor_tensor(dst, X, bc(rstd), ALU.mult).then_inc(done, 1)

            def layer(b, l):
                n = b * LAYERS + l
                for g in range(NC):
                    q = slice(CT * g, CT * g + CT)
                    wxm = wx[g % 2][0:P, :].rearrange("p (t c) -> p t c", t=CT)[:, :, F:2 * F]
                    dve.wait_ge(self_done, n * NC + g + 1)
                    if g >= 1:
                        dve.wait_ge(m3_done, n * NC + g)
                    v.tensor_tensor(TMP[:, q, :], wxm, M3[:, q, 0:F], ALU.subtract).then_inc(m3_step, 1)
                    dve.wait_ge(m3_step, (n * NC + g) * 2 + 1)
                    v.tensor_copy(M3[:, q, F:2 * F], TMP[:, q, :]).then_inc(m3_step, 1)
                    dve.wait_ge(m3_step, (n * NC + g) * 2 + 2)
                    v.tensor_tensor(M3[:, q, 2 * F:3 * F], TMP[:, q, :], M3[:, q, F:2 * F], ALU.subtract
                                    ).then_inc(m3_done, 1)
                for q in range(T // 2):
                    m = n * (T // 2) + q + 1
                    dve.wait_ge(acc_full, m)
                    v.tensor_reduce(TMP[:, 2 * q:2 * q + 2, :],
                                    pAcc[0:P, q % 4, 0:6 * F].rearrange("p (t a f) -> p t f a", t=2, a=3),
                                    AX.X, ALU.add).then_inc(acc_done, 1)
                    dve.wait_ge(acc_done, m)
                    v.tensor_tensor(HC[:, 2 * q:2 * q + 2, :], TMP[:, 2 * q:2 * q + 2, :],
                                    SELF[:, 2 * q:2 * q + 2, :], ALU.add).then_inc(add_done, 1)
                dve.wait_ge(add_done, (n + 1) * (T // 2))
                v.tensor_scalar(HC, HC, floor[:, bass.ds(l, 1)], None, ALU.max).then_inc(hc_ready, 1)

            wx = (pO, misc)
            with dve.Fori(0, B) as b:
                prologue(b)
                region(b, 0, True, False)
                with dve.Fori(1, NC) as k:
                    region(b, k, True, True)
                region(b, NC, False, True)
                dve.wait_ge(x_res, (b + 1) * 16)
                dve.wait_ge(fin, (b + 1) * (5 * NC))
                layernorm(b * 16, b * 2 + 1, H0[:, :, :], HC, hc_ready)
                with dve.Fori(0, LAYERS) as l:
                    layer(b, l)
                dve.wait_ge(x1_done, b + 1)
                dve.wait_ge(hc_ready, (b + 1) * (LAYERS + 1))
                layernorm(b * 16 + 8, b * 2 + 2, HC, HC, y_done)

        @block.scalar
        def _(act):
            cp = nc.scalar.copy
            act.wait_ge(consts, N_CONST)
            act.wait_ge(w_turned, 1)
            cp(W3[0:F, :, :], pA[0:F, 0, 0:2 * F * LAYERS].rearrange("p (l c) -> p l c", l=LAYERS)
               ).then_inc(w_placed, 1)

            def prologue(b):
                for c in range(NC + 1):
                    if c < NC:
                        act.wait_ge(x_turned, chunks(b, c) + 1)
                        if c >= 2:
                            act.wait_ge(val_full, chunks(b, c) - 1)
                        cp(xT[:, c % 2, :], pA[0:F, c % 2, 0:C]).then_inc(x_sb, 1)
                    if c >= 1:
                        d = c - 1
                        act.wait_ge(proj_full, chunks(b, d) + 1)
                        if d >= 2:
                            act.wait_ge(scr_out[d % 2], (b * (NC // 2) + d // 2) * 16)
                        cp(parts[:, d % 2, 0, :], pB[:, 0, d % 2, 0:C]).then_inc(high_done, 1)
                        act.wait_ge(val_full, chunks(b, d) + 1)
                        cp(VA[:, CT * d:CT * d + CT, :, 0:D],
                           pB[0:P, 1, d % 2, 0:CT * F].rearrange("p (t h d) -> p t h d", t=CT, h=H)
                           ).then_inc(val_done, 1)

            def empty(b, k, kind, i):
                act.wait_ge(misc_full, turns(b, k) + TURN_OF[kind, i] + 1)
                if kind == "mask":
                    t, j = i // NJ, i % NJ
                    cp(MT[:, k % 2, BPP * j:BPP * j + BPP, P * t:P * t + P], misc16[0:P, :, 0:P]
                       ).then_inc(misc_done, 1)
                else:
                    cp(FQ[KS:KX, k % 2, :, P * i:P * i + P], misc16[KS:KX, 0:H, 0:P]).then_inc(misc_done, 1)

            def exp_b(b, k, u, both):
                act.wait_ge(sx_full, chunks(b, k) * UNITS + u + 1)
                if u >= 4:
                    act.wait_ge(pv_done, chunks(b, k) * T + u // 2 - 1)
                nc.scalar.activation(banks(E[0:P, u % 4, :]), bank_b(both, u)[0:P, :, 0:C], ACT.Exp, scale=0.2
                                     ).then_inc(exp_done, 1)

            def region(b, k, a, bb_):
                lag = LAG if a and bb_ else 0
                plan = list(PLAN) if a else []
                for s in range(UNITS + 4):
                    if bb_ and 1 <= s <= UNITS:
                        exp_b(b, k - 1, s - 1, a)
                    while plan and plan[0][0] <= s - lag:
                        empty(b, k, *plan.pop(0)[1:])
                if bb_:
                    act.wait_ge(pv_done, (chunks(b, k - 1) + 1) * T)
                    for h in range(H):
                        cp(OT[32 * h:32 * h + V, :], pO[32 * h:32 * h + V, 0:C]).then_inc(ot_done, 1)
                for _, kind, i in plan:
                    empty(b, k, kind, i)
                if bb_:
                    act.wait_ge(misc_full, turns(b, k) + (MISC_A if a else 0) + 1)
                    cp(ON[:, :, :, :], misc[0:P, :].rearrange("p (t h v) -> p t h v", t=CT, h=H)[:, :, :, 0:V]
                       ).then_inc(misc_done, 1)

            def root(n, m):
                act.wait_ge(ln, n + 7)
                nc.scalar.activation(std[:, :], var[:, :], ACT.Sqrt).then_inc(std_done, 1)

            wx = (pO, misc)

            def layer(b, l):
                n = b * LAYERS + l
                for g in range(NC + 1):
                    if g < NC:
                        act.wait_ge(ht_full, n * NC + g + 1)
                        cp(HT[0:F, C * g:C * g + C], pA[0:F, g % 2, 0:C]).then_inc(ht_done, 1)
                    if g >= 1:
                        d = g - 1
                        q = slice(CT * d, CT * d + CT)
                        w = wx[d % 2][0:P, :].rearrange("p (t c) -> p t c", t=CT)
                        act.wait_ge(wx_full, n * NC + d + 1)
                        cp(M3[:, q, 0:F], w[:, :, F:2 * F])
                        cp(SELF[:, q, :], w[:, :, 0:F]).then_inc(self_done, 1)

            with act.Fori(0, B) as b:
                prologue(b)
                region(b, 0, True, False)
                with act.Fori(1, NC) as k:
                    region(b, k, True, True)
                region(b, NC, False, True)
                root(b * 16, 0)
                act.wait_ge(hc_ready, b * (LAYERS + 1) + 1)
                cp(X, HC).then_inc(x1_done, 1)
                with act.Fori(0, LAYERS) as l:
                    layer(b, l)
                root(b * 16 + 8, 1)

        @block.gpsimd
        def _(pool):
            g = nc.gpsimd
            g.memset(ident[:, :], 0.0).then_inc(ident_step, 1)
            pool.wait_ge(ident_step, 1)
            g.affine_select(out=ident[:, :], in_=ident[:, :], compare_op=ALU.not_equal, fill=1.0, base=0,
                            pattern=[[-1, 128]], channel_multiplier=1).then_inc(ident_step, 1)
            pool.wait_ge(ident_step, 2)
            g.tensor_copy(ident16[:, :], ident[:, :]).then_inc(ident_step, 1)

            def quarter(b, k):
                pool.wait_ge(fs_in, (chunks(b, k) + 1) * 96)
                if k >= 2:
                    pool.wait_ge(sx_full, chunks(b, k - 1) * UNITS)
                apart(pool)
                g.tensor_scalar(FQ[0:KS, k % 2, :, :], FS[:, k % 3, :, :], 0.25, 1.0, ALU.mult, ALU.mult
                                ).then_inc(fq_ready, 1)

            def mask(b, k, p):
                pool.wait_ge(a_in[p % 2], (chunks(b, k) * (PIECES // 2) + p // 2 + 1) * 16)
                if p >= 3:
                    pool.wait_ge(max_done, chunks(b, k) * UNITS + (p - 2) * H + 1)
                    pool.wait_ge(misc_full, turns(b, k) + TURN_OF["mask", p - 3] + 1)
                elif k >= 1:
                    pool.wait_ge(max_done, chunks(b, k - 1) * UNITS + (p - 2 + PIECES) * H + 1)
                    pool.wait_ge(misc_full, turns(b, k - 1) + TURN_OF["mask", p - 3 + PIECES] + 1)
                apart(pool)
                g.tensor_scalar(M16[:, p % 3, :], A32[:, p % 2, :], -1.0, BIG, ALU.add, ALU.mult
                                ).then_inc(m16_ready, 1)

            def adjacency8(b, k, t):
                pool.wait_ge(misc_done, turns(b, k) + TURN_OF["mask", NJ * t + NJ - 1] + 2)
                q = C * k + P * t
                apart(pool)
                g.tensor_scalar(AT[:, :, q:q + P], MT[:, k % 2, :, P * t:P * t + P], ONE8 / BIG, ONE8,
                                ALU.mult, ALU.add).then_inc(at_done, 1)

            with pool.Fori(0, B) as b:
                for k in range(NC):
                    quarter(b, k)
                    for p in range(PIECES):
                        mask(b, k, p)
                        if p % NJ == NJ - 1 and p >= 2 * NJ - 1:
                            adjacency8(b, k, p // NJ - 1)
                    adjacency8(b, k, CT - 1)


_INS = ["x", "adj", "L0_gnn_kernel", "L0_gnn_attention_kernel", "L0_gnn_attention_kernel_2", "L0_gnn_bias",
        "L1_gnn_Wm0", "L1_gnn_Ws0", "L1_gnn_b0", "L1_gnn_Wm1", "L1_gnn_Ws1", "L1_gnn_b1",
        "L1_gnn_Wm2", "L1_gnn_Ws2", "L1_gnn_b2"]


def kernel(**inputs):
    import concourse.bacc as bacc
    import numpy as np
    from concourse.bass_utils import run_bass_kernel_spmd

    nc = bacc.Bacc("TRN2", target_bir_lowering=False, num_devices=1, dynamic_dma_scratch_size=1024)
    arrays, args = {}, {}
    for name in _INS:
        a = np.ascontiguousarray(inputs[name])
        arrays[f"in_{name}"] = a
        args[name] = nc.dram_tensor(f"in_{name}", a.shape, mybir.dt.from_np(a.dtype), kind="ExternalInput").ap()
    out = nc.dram_tensor("out_0", (B, N, F), F32, kind="ExternalOutput").ap()
    build(nc, args["x"], args["adj"], args["L0_gnn_kernel"], args["L0_gnn_attention_kernel"],
          args["L0_gnn_attention_kernel_2"], args["L0_gnn_bias"],
          [args[f"L1_gnn_Wm{l}"] for l in range(LAYERS)], [args[f"L1_gnn_Ws{l}"] for l in range(LAYERS)],
          [args[f"L1_gnn_b{l}"] for l in range(LAYERS)], out)
    r = run_bass_kernel_spmd(nc, [arrays], core_ids=[0])
    return r.results[0]["out_0"]
```

```python
from contextlib import ExitStack

import concourse.bass as bass
from concourse import mybir

F32 = mybir.dt.float32
BF16 = mybir.dt.bfloat16
FP8 = mybir.dt.float8e4
U8 = mybir.dt.uint8
ALU = mybir.AluOpType
ACT = mybir.ActivationFunctionType
AX = mybir.AxisListType

B, N, F = 8, 3000, 64
H, D = 4, 16
HD = H * D
P = 125
T = N // P
CT = 4
C = CT * P
NC = N // C
PIECE = 2 * C
NJ = N // PIECE
BPP = PIECE // P
LAYERS = 3
PAIRS = H // 2
KS = 6 * D
KX = KS + 2
V = D + 1
UNITS = CT * NJ * H
assert UNITS == T * PAIRS
PIECES = CT * NJ
LAG = 5
BIG = 2.0 ** 35
ONE8 = 56.0
EPS = 1e-5
NEG = -3.0e38
PART_S = (0, 0, 1, 1, 0, 2)
PART_O = (0, 1, 0, 1, 2, 0)


def turn_plan():
    plan = [(4 * p + 1, "mask", p, 0) for p in range(PIECES)]
    for t in range(CT):
        step = (t + 1) * NJ * H + 4
        plan.append((step % UNITS, "shift", t, step // UNITS))
    plan.append((LAG + 5, "result", 0, 2))
    return sorted(plan)


PLAN = turn_plan()
assert PLAN[-1][1:] == ("mask", PIECES - 1, 0)


def back(k, n):
    return k - n if isinstance(k, int) else (k[0], k[1] - n)


def exists(k):
    return not isinstance(k, int) or 0 <= k < NC


def slot(k, n):
    return k % n if isinstance(k, int) else (k[0] + k[1] % n) % n


def upto(b, k, per, i):
    if isinstance(k, int):
        return b * (NC * per) + (k * per + i)
    return (b * NC + k[0]) * per + (k[1] * per + i)


def upto_b(b, k, per, i):
    if isinstance(k, int):
        return (b * NC + k) * per + i
    return (b * NC + k[0]) * per + (k[1] * per + i)


def first_tile(k):
    return k * CT if isinstance(k, int) else k[0] * CT + k[1] * CT


def plan_of(k):
    return [t for t in PLAN if exists(back(k, t[3]))]


def unit_b(k, x):
    c, u = (back(k, 1), x) if x >= 0 else (back(k, 2), x + UNITS)
    return (c, u) if exists(c) else (None, -1)


def build(nc, x, adj, kernel, att1, att2, bias, wm, ws, bb, out):
    scratch = nc.dram_tensor("scratch", (3, 2 * HD, N), BF16, kind="Internal").ap()

    with ExitStack() as ctx:
        def sb(name, shape, dt):
            return ctx.enter_context(nc.sbuf_tensor(name, shape, dt))

        def psum(name, shape, dt):
            return ctx.enter_context(nc.psum_tensor(name, shape, dt))

        def sem(name):
            return ctx.enter_context(nc.semaphore(name))

        AT = sb("AT", [P, T, N], U8)
        MT = sb("MT", [P, 2, T, C], BF16)
        FO = sb("FO", [KX, H, N], BF16)
        FS = sb("FS", [KS, 3, H, C], BF16)
        FQ = sb("FQ", [KX, 2, H, C], BF16)
        A32 = sb("A32", [P, 2, PIECE], F32)
        M16 = sb("M16", [P, 3, PIECE], BF16)
        E = sb("E", [128, 4, PIECE], F32)
        VA = sb("VA", [P, T, H, V], F32)
        OT = sb("OT", [128, C], F32)
        ON = sb("ON", [P, CT, H, V], F32)
        H0 = sb("H0", [P, T, HD], F32)
        ident = sb("ident", [128, 128], F32)
        ident16 = sb("ident16", [128, 128], BF16)
        cm = sb("cm", [P, 2, H, NJ], F32)
        mx = sb("mx", [P, H], F32)
        sh = sb("sh", [P, H], F32)
        sh2 = sb("sh2", [P, H], F32)
        shift = sb("shift", [P, H, 2], BF16)
        den = sb("den", [P, CT, H], F32)
        rden = sb("rden", [P, CT, H], F32)
        wqk = sb("wqk", [F, 2 * HD], F32)
        wv = sb("wv", [F, HD], F32)
        biasb = sb("biasb", [P, HD], F32)
        HT = sb("HT", [F + 1, N], F32)
        W3 = sb("W3", [F + 1, LAYERS, 2 * F], F32)
        floor = sb("floor", [P, LAYERS], F32)
        mean = sb("mean", [P, T], F32)
        var = sb("var", [P, T], F32)
        std = sb("std", [P, T], F32)
        rstd = sb("rstd", [P, T], F32)

        work = MT[:, :, :, :].rearrange("p a t c -> p (a t c)").bitcast(F32)
        TF = T * F
        X = work[:, 0:TF].rearrange("p (t f) -> p t f", f=F)
        HC = work[:, TF:2 * TF].rearrange("p (t f) -> p t f", f=F)
        SELF = work[:, 2 * TF:3 * TF].rearrange("p (t f) -> p t f", f=F)
        TMP = work[:, 3 * TF:4 * TF].rearrange("p (t f) -> p t f", f=F)
        M3 = work[:, 4 * TF:4 * TF + T * 3 * F // 2].bitcast(BF16).rearrange("p (t c) -> p t c", c=3 * F)
        assert 4 * TF + T * 3 * F // 2 <= T * C
        free = E[:, :, :].rearrange("p s c -> p (s c)")
        xin = free[0:P, 0:2 * CT * F].rearrange("p (s t f) -> p s t f", s=2, f=F)
        at = 2 * CT * F
        xT = free[0:F, at:at + 2 * C].rearrange("p (s c) -> p s c", s=2)
        at += 2 * C
        rest = free[:, at:at + C]
        at += C
        parts = free[:, at:at + 3 * C].bitcast(BF16).rearrange("p (s a c) -> p s a c", s=2, a=3)
        assert at + 3 * C <= 4 * PIECE and 2 * HD == 128

        pA = psum("pA", [128, 2, 512], F32)
        pB = psum("pB", [128, 2, 2, 512], F32)
        pO = psum("pO", [128, 512], F32)
        misc = psum("misc", [128, 512], F32)
        misc16 = misc[:, :].bitcast(BF16).rearrange("p (b c) -> p b c", c=128)
        pAcc = pB[:, :, :, :].rearrange("p a b c -> p (a b) c")
        wx = (pB[:, 0, 0, :], pB[:, 0, 1, :])

        w_loaded = sem("w_loaded")
        consts = sem("consts")
        ident_step = sem("ident_step")
        w_turned = sem("w_turned")
        w_placed = sem("w_placed")
        x_in = [sem("x_in0"), sem("x_in1")]
        x_turned = sem("x_turned")
        x_sb = sem("x_sb")
        proj_full = sem("proj_full")
        val_full = sem("val_full")
        high_done = sem("high_done")
        val_done = sem("val_done")
        rest_done = sem("rest_done")
        mid_done = sem("mid_done")
        parts_done = sem("parts_done")
        scr_out = [sem("scr_out0"), sem("scr_out1")]
        fo_in = sem("fo_in")
        fs_in = sem("fs_in")
        a_in = [sem("a_in0"), sem("a_in1")]
        m16_ready = sem("m16_ready")
        fq_ready = sem("fq_ready")
        sn_full = sem("sn_full")
        max_done = sem("max_done")
        stat = sem("stat")
        shift_done = sem("shift_done")
        turned = {"mask": sem("mask_turned"), "shift": sem("shift_turned"), "result": sem("result_turned")}
        placed = {"mask": sem("mask_placed"), "shift": sem("shift_placed"), "result": sem("result_placed")}
        at_done = sem("at_done")
        sm_full = sem("sm_full")
        relu_done = sem("relu_done")
        sx_full = sem("sx_full")
        exp_done = sem("exp_done")
        pv_done = sem("pv_done")
        ot_done = sem("ot_done")
        fin = sem("fin")
        x_res = sem("x_res")
        ln = sem("ln")
        std_done = sem("std_done")
        x1_done = sem("x1_done")
        hc_ready = sem("hc_ready")
        ht_full = sem("ht_full")
        ht_done = sem("ht_done")
        wx_full = sem("wx_full")
        self_done = sem("self_done")
        m3_step = sem("m3_step")
        m3_done = sem("m3_done")
        acc_full = sem("acc_full")
        acc_done = sem("acc_done")
        add_done = sem("add_done")
        y_done = sem("y_done")
        y_out = sem("y_out")
        passed = sem("passed")

        x_v = x.rearrange("b (t p) f -> b p t f", p=P)
        out_v = out.rearrange("b (t p) f -> b p t f", p=P)
        adj_v = adj.rearrange("b (t p) (j c) -> b t j p c", p=P, c=PIECE)
        scr_v = scratch.rearrange("a p n -> p a n")
        id_p = ident[0:P, 0:P]
        id16 = ident16[0:P, 0:P]

        def banks(ap):
            return ap.rearrange("p (a c) -> p a c", a=2)

        def bank_a(k, u):
            alone = isinstance(k, int) and k == 0
            return (pA[:, :, :], pB[:, 0, :, :], pB[:, 1, :, :])[u % 3 if alone else 0]

        def last_chunk(k):
            return isinstance(k, int) and k == NC - 1

        def bank_b(k, u):
            return (pB[:, 0, :, :], pB[:, 1, :, :], pA[:, :, :])[u % 3 if last_chunk(k) else u % 2]

        PER_CHUNK = {"mask": PIECES, "shift": CT, "result": 1}

        def nth(b, k, kind, i):
            return upto(b, k, PER_CHUNK[kind], i + 1)

        N_CONST = 8

        def apart(eng):
            eng.sem_inc(passed, 1)

        block = ctx.enter_context(nc.Block())

        @block.sync
        def _(sp):
            for dst, src in ((wqk[:, 0:HD], att1), (wqk[:, HD:2 * HD], att2), (wv[:, :], kernel)):
                sp.dma_start(dst.rearrange("f (h d) -> f h d", h=H), src.rearrange("h f d -> f h d")
                             ).then_inc(w_loaded, 16)
            sp.dma_start(biasb[:, :], bias.rearrange("a b h d -> (a b h d)").partition_broadcast(P)
                         ).then_inc(w_loaded, 16)
            for l in range(LAYERS):
                sp.dma_start(SELF[0:F, l, :], ws[l]).then_inc(w_loaded, 16)
                sp.dma_start(TMP[0:F, l, :], wm[l]).then_inc(w_loaded, 16)
            sp.wait_ge(consts, N_CONST)
            for l in range(LAYERS):
                sp.dma_start(W3[F:F + 1, l, 0:F], bb[l].unsqueeze(0)).then_inc(w_loaded, 16)

            def load_x(b, c):
                if c >= 2:
                    sp.wait_ge(x_turned, upto(b, c, 1, -1))
                    apart(sp)
                sp.dma_start(xin[:, c % 2, :, :], x_v[b, :, CT * c:CT * c + CT, :]
                             ).then_inc(x_in[c % 2], 16)

            def load_queries(k, slot):
                for g in range(6):
                    sp.dma_start(FS[D * g:D * g + D, slot, :, :],
                                 scratch[PART_S[g], 0:HD, bass.ds(k * C, C)].rearrange(
                                     "(h d) n -> d h n", h=H)).then_inc(fs_in, 16)

            def load_rows(b, k):
                for p in range(PIECES):
                    sp.wait_ge(m16_ready, upto(b, k, PIECES, p + 1))
                    apart(sp)
                    sp.dma_start(A32[:, p % 2, :], adj_v[b, first_tile(k) + p // NJ, p % NJ]
                                 ).then_inc(a_in[p % 2], 16)

            with sp.Fori(0, B) as b:
                sp.wait_ge(y_done, b + 1)
                apart(sp)
                load_x(b, 0)
                load_x(b, 1)
                for c in range(NC):
                    sp.wait_ge(parts_done, upto(b, c, 1, 1))
                    apart(sp)
                    sp.dma_start(scr_v[:, :, C * c:C * c + C], parts[:, c % 2, :, :]
                                 ).then_inc(scr_out[c % 2], 16)
                    if c + 2 < NC:
                        load_x(b, c + 2)
                for s in scr_out:
                    sp.wait_ge(s, (b + 1) * (16 * NC // 2))
                apart(sp)
                for g in range(6):
                    sp.dma_start(FO[D * g:D * g + D, :, :],
                                 scratch[PART_O[g], HD:2 * HD, :].rearrange("(h d) n -> d h n", h=H)
                                 ).then_inc(fo_in, 16)
                load_queries(0, 0)
                load_rows(b, 0)
                load_queries(1, 1)
                load_rows(b, 1)
                load_queries(2, 2)
                with sp.Fori(2, NC - 1) as k:
                    load_rows(b, (k, 0))
                    sp.wait_ge(sm_full, upto(b, (k, -1), UNITS, 0))
                    apart(sp)
                    load_queries(k + 1, (k + 1) % 3)
                load_rows(b, NC - 1)
                sp.wait_ge(relu_done, (b + 1) * (NC * UNITS))
                apart(sp)
                sp.wait_ge(at_done, (b + 1) * T)
                apart(sp)
                sp.dma_start(X, x_v[b]).then_inc(x_res, 16)
                sp.wait_ge(y_done, b + 2)
                apart(sp)
                sp.dma_start(out_v[b], HC).then_inc(y_out, 16)
                sp.wait_ge(y_out, (b + 1) * 16)
                apart(sp)

        @block.tensor
        def _(pe):
            mm = nc.tensor.matmul

            pe.wait_ge(ident_step, 3)
            pe.wait_ge(w_loaded, 16 * (4 + 3 * LAYERS))
            for l in range(LAYERS):
                for o, w in ((0, SELF), (F, TMP)):
                    last = nc.tensor.transpose(pA[0:F, 0, 2 * F * l + o:2 * F * l + o + F], w[0:F, l, :],
                                               ident[0:F, 0:F])
            last.then_inc(w_turned, 1)
            pe.wait_ge(w_placed, 1)

            def prologue(b):
                for c in range(NC + 1):
                    if c < NC:
                        pe.wait_ge(x_in[c % 2], (b * (NC // 2) + c // 2 + 1) * 16)
                        if c >= 2:
                            pe.wait_ge(x_sb, upto(b, c, 1, -1))
                        apart(pe)
                        for t in range(CT):
                            last = nc.tensor.transpose(pA[0:F, c % 2, P * t:P * t + P], xin[:, c % 2, t, :],
                                                       id_p)
                        last.then_inc(x_turned, 1)
                    if c >= 1:
                        d = c - 1
                        pe.wait_ge(x_sb, upto(b, d, 1, 1))
                        if d >= 2:
                            pe.wait_ge(rest_done, upto(b, d, 1, -1))
                            pe.wait_ge(val_done, upto(b, d, 1, -1))
                        mm(pB[:, 0, d % 2, 0:C], wqk[:, :], xT[:, d % 2, :], start=True, stop=True
                           ).then_inc(proj_full, 1)
                        for t in range(CT):
                            last = mm(pB[0:P, 1, d % 2, F * t:F * t + F], xT[:, d % 2, P * t:P * t + P],
                                      wv[:, :], start=True, stop=True)
                        last.then_inc(val_full, 1)

            def scores_a(b, k, u):
                t, j, h = u // (NJ * H), u // H % NJ, u % H
                if u == 0:
                    pe.wait_ge(fs_in, upto(b, k, 96, 96))
                if not (isinstance(k, int) and k == 0):
                    pe.wait_ge(max_done, upto(b, k, UNITS, u + 1))
                elif u >= 3:
                    pe.wait_ge(max_done, upto(b, k, UNITS, u - 1))
                for a in range(2):
                    last = mm(bank_a(k, u)[0:P, a, 0:C], FS[:, slot(k, 3), h, P * t:P * t + P],
                              FO[0:KS, h, PIECE * j + C * a:PIECE * j + C * a + C], start=True, stop=True)
                last.then_inc(sn_full, 1)

            def turn(b, k, n):
                plan = plan_of(k)
                _, kind, i, ago = plan[n]
                if n > 0:
                    _, before, j, c = plan[n - 1]
                    pe.wait_ge(placed[before], nth(b, back(k, c), before, j))
                elif not (isinstance(k, int) and k == 0):
                    _, before, j, c = plan_of(back(k, 1))[-1]
                    pe.wait_ge(placed[before], nth(b, back(k, 1 + c), before, j))
                if kind == "mask":
                    pe.wait_ge(m16_ready, upto(b, k, PIECES, i + 3))
                    for s in range(BPP):
                        last = nc.tensor.transpose(misc16[0:P, s, 0:P], M16[:, i % 3, P * s:P * s + P], id16)
                elif kind == "shift":
                    pe.wait_ge(shift_done, nth(b, back(k, ago), "shift", i))
                    for h in range(H):
                        last = nc.tensor.transpose(misc16[KS:KX, h, 0:P], shift[:, h, :], id16)
                else:
                    pe.wait_ge(ot_done, nth(b, back(k, ago), "result", i))
                    apart(pe)
                    for t in range(CT):
                        last = nc.tensor.transpose(misc[0:P, 128 * t:128 * t + 128], OT[:, P * t:P * t + P],
                                                   ident[:, :])
                last.then_inc(turned[kind], 1)

            def scores_b(b, k, u):
                i, pair = u // PAIRS, u % PAIRS
                if not last_chunk(k) or u < 2:
                    pe.wait_ge(exp_done, upto_b(b, k, UNITS, u + 1))
                elif u == 2:
                    pe.wait_ge(max_done, upto(b, NC, UNITS, 1))
                else:
                    pe.wait_ge(exp_done, upto_b(b, k, UNITS, u))
                for a in range(2):
                    h = 2 * pair + a
                    last = mm(bank_b(k, u)[0:P, a, 0:C], FO[0:KS, h, P * i:P * i + P], FS[:, slot(k, 3), h, :],
                              start=True, stop=True)
                last.then_inc(sm_full, 1)

            def exponent_b(b, k, u):
                i, pair = u // PAIRS, u % PAIRS
                if u == 0:
                    pe.wait_ge(fq_ready, upto(b, k, 1, 1))
                    pe.wait_ge(placed["shift"], nth(b, k, "shift", CT - 1))
                pe.wait_ge(relu_done, upto_b(b, k, UNITS, u + 1))
                for a in range(2):
                    h = 2 * pair + a
                    last = mm(bank_b(k, u)[0:P, a, 0:C], FO[0:KX, h, P * i:P * i + P], FQ[:, slot(k, 2), h, :],
                              start=False, stop=True, skip_group_check=True)
                last.then_inc(sx_full, 1)

            def values_b(b, k, i):
                pe.wait_ge(exp_done, upto_b(b, k, UNITS, 2 * i + 4))
                if i == 0 and not (isinstance(k, int) and k == 0):
                    pe.wait_ge(ot_done, upto(b, k, 1, 0))
                for h in range(H):
                    last = mm(pO[32 * h:32 * h + V, 0:C], VA[:, i, h, :],
                              E[0:P, (2 * i + h // 2) % 4, C * (h % 2):C * (h % 2) + C],
                              start=(i == 0), stop=(i == T - 1))
                last.then_inc(pv_done, 1)

            def body(b, k, steps=UNITS):
                plan = plan_of(k)
                n = 0
                for r in range(steps):
                    c, u = unit_b(k, r - LAG - 2)
                    if c is not None:
                        exponent_b(b, c, u)
                    c, u = unit_b(k, r - LAG - 5)
                    if c is not None and u % 2 == 0:
                        values_b(b, c, u // 2)
                    if exists(k) and r < UNITS:
                        scores_a(b, k, r)
                    while n < len(plan) and plan[n][0] == r:
                        turn(b, k, n)
                        n += 1
                    c, u = unit_b(k, r - LAG)
                    if c is not None:
                        scores_b(b, c, u)

            def layer(b, l):
                n = b * LAYERS + l
                pe.wait_ge(hc_ready, b * (LAYERS + 1) + l + 1)
                for g in range(NC + 1):
                    if g < NC:
                        if g >= 2:
                            pe.wait_ge(ht_done, n * NC + g - 1)
                        apart(pe)
                        for t in range(CT):
                            last = nc.tensor.transpose(pA[0:F, g % 2, P * t:P * t + P], HC[:, CT * g + t, :],
                                                       id_p)
                        last.then_inc(ht_full, 1)
                    if g >= 1:
                        d = g - 1
                        pe.wait_ge(ht_done, n * NC + d + 1)
                        if d >= 2:
                            pe.wait_ge(m3_done, n * NC + d - 1)
                            pe.wait_ge(self_done, n * NC + d - 1)
                        for t in range(CT):
                            q = C * d + P * t
                            last = mm(wx[d % 2][0:P, 2 * F * t:2 * F * t + 2 * F], HT[:, q:q + P],
                                      W3[:, l, :], start=True, stop=True)
                        last.then_inc(wx_full, 1)
                pe.wait_ge(m3_done, (n + 1) * NC)
                apart(pe)
                for t in range(T):
                    if t % 2 == 0 and t >= 8:
                        pe.wait_ge(acc_done, n * (T // 2) + t // 2 - 3)
                        apart(pe)
                    for i in range(T):
                        last = mm(pAcc[0:P, t // 2 % 4, 3 * F * (t % 2):3 * F * (t % 2) + 3 * F],
                                  AT[:, i, P * t:P * t + P].bitcast(FP8), M3[:, i, :],
                                  start=(i == 0), stop=(i == T - 1))
                    if t % 2:
                        last.then_inc(acc_full, 1)

            with pe.Fori(0, B) as b:
                prologue(b)
                pe.wait_ge(rest_done, upto(b, NC, 1, 0))
                pe.wait_ge(val_done, upto(b, NC, 1, 0))
                pe.wait_ge(fo_in, (b + 1) * 96)
                body(b, 0)
                body(b, 1)
                with pe.Fori(2, NC) as k:
                    body(b, (k, 0))
                body(b, NC)
                body(b, NC + 1, LAG + 6)
                with pe.Fori(0, LAYERS) as l:
                    layer(b, l)

        @block.vector
        def _(dve):
            v = nc.vector
            v.memset(FO[KS:KX, :, :], 1.0).then_inc(consts, 1)
            v.memset(VA[:, :, :, :], 1.0).then_inc(consts, 1)
            v.memset(OT[:, :], 0.0).then_inc(consts, 1)
            v.memset(pO[:, :], 0.0).then_inc(consts, 1)
            v.memset(W3[:, :, :], 0.0).then_inc(consts, 1)
            v.memset(HT[F:F + 1, :], 1.0).then_inc(consts, 1)
            v.memset(floor[:, 0:LAYERS - 1], 0.0).then_inc(consts, 1)
            v.memset(floor[:, LAYERS - 1:LAYERS], NEG).then_inc(consts, 1)
            dve.sem_inc(max_done, 1)
            dve.sem_inc(y_done, 1)
            dve.sem_inc(exp_done, 2)
            dve.sem_inc(m16_ready, 2)
            dve.wait_ge(consts, N_CONST)

            def prologue(b):
                for c in range(NC):
                    n = upto(b, c, 1, 1)
                    dve.wait_ge(high_done, n)
                    if c >= 1:
                        dve.wait_ge(parts_done, n - 1)
                    v.tensor_tensor(rest, pB[:, 0, c % 2, 0:C], parts[:, c % 2, 0, :], ALU.subtract
                                    ).then_inc(rest_done, 1)
                    dve.wait_ge(rest_done, n)
                    v.tensor_copy(parts[:, c % 2, 1, :], rest).then_inc(mid_done, 1)
                    dve.wait_ge(mid_done, n)
                    v.tensor_tensor(parts[:, c % 2, 2, :], rest, parts[:, c % 2, 1, :], ALU.subtract
                                    ).then_inc(parts_done, 1)

            def maximum_a(b, k, u):
                p, h = u // H, u % H
                if h == 0:
                    dve.wait_ge(m16_ready, upto(b, k, PIECES, p + 3))
                dve.wait_ge(sn_full, upto(b, k, UNITS, u + 1))
                apart(dve)
                pu = bank_a(k, u)[0:P, :, 0:C]
                v.tensor_tensor_reduce(pu, pu, banks(M16[:, p % 3, :]), 1.0, NEG,
                                       ALU.add, ALU.max, cm[:, p // NJ % 2, h, p % NJ:p % NJ + 1]).then_inc(max_done, 1)

            def shift_step(b, k, t, i):
                n = nth(b, k, "shift", t) * 4 - 4
                if i == 0:
                    dve.wait_ge(max_done, upto(b, k, UNITS, (t + 1) * NJ * H + 1))
                    v.tensor_reduce(mx[:, :], cm[:, t % 2, :, :], AX.X, ALU.max).then_inc(stat, 1)
                else:
                    dve.wait_ge(stat, n + i)
                if i == 1:
                    v.tensor_scalar(sh2[:, :], mx[:, :], -1.25, None, ALU.mult).then_inc(stat, 1)
                if i == 2:
                    v.scalar_tensor_tensor(out=sh[:, :], in0=mx[:, :], scalar=-0.25, op0=ALU.mult,
                                           in1=sh2[:, :], op1=ALU.min).then_inc(stat, 1)
                if i == 3:
                    v.tensor_copy(shift[:, :, 0], sh[:, :]).then_inc(stat, 1)
                if i == 4:
                    v.tensor_tensor(shift[:, :, 1], sh[:, :], shift[:, :, 0], ALU.subtract
                                    ).then_inc(shift_done, 1)

            def relu_b(b, k, u):
                if u == 0:
                    dve.wait_ge(placed["mask"], nth(b, k, "mask", PIECES - 1))
                dve.wait_ge(sm_full, upto(b, k, UNITS, u + 1))
                i = u // PAIRS
                pu = bank_b(k, u)[0:P, :, 0:C]
                v.scalar_tensor_tensor(out=pu, in0=pu, scalar=0.0, op0=ALU.max,
                                       in1=MT[:, slot(k, 2), i, :].unsqueeze(1).broadcast_to([P, 2, C]),
                                       op1=ALU.add).then_inc(relu_done, 1)

            def finish_step(b, k, i):
                h0 = H0[:, bass.ds(first_tile(k), CT), :]
                h04 = h0.rearrange("p t (h d) -> p t h d", h=H)
                if i == 0:
                    dve.wait_ge(placed["result"], nth(b, k, "result", 0))
                    v.tensor_scalar(den[:, :, :], ON[:, :, :, D], 1e-30, None, ALU.max).then_inc(fin, 1)
                else:
                    dve.wait_ge(fin, upto(b, k, 5, i))
                if i == 1:
                    v.reciprocal(rden[:, :, :], den[:, :, :]).then_inc(fin, 1)
                if i == 2:
                    v.tensor_tensor(h04, ON[:, :, :, 0:D],
                                    rden[:, :, :].unsqueeze(3).broadcast_to([P, CT, H, D]),
                                    ALU.mult).then_inc(fin, 1)
                if i == 3:
                    v.tensor_tensor(h0, h0, biasb[:, :].unsqueeze(1).broadcast_to([P, CT, HD]), ALU.add
                                    ).then_inc(fin, 1)
                if i == 4:
                    v.tensor_scalar(h0, h0, 0.0, None, ALU.max).then_inc(fin, 1)

            def body(b, k, steps=UNITS):
                for r in range(steps):
                    since, t = (r + 1) % (NJ * H), (r + 1) // (NJ * H) - 1
                    c = k if t >= 0 else back(k, 1)
                    small = [2 * since - 1, 2 * since] if since <= 2 and exists(c) else []
                    if exists(k) and r < UNITS:
                        maximum_a(b, k, r)
                    if small and small[0] >= 1 and r < UNITS:
                        shift_step(b, c, t % CT, small[0])
                    c2, u = unit_b(k, r - LAG)
                    if c2 is not None:
                        relu_b(b, c2, u)
                    if small and r < UNITS:
                        shift_step(b, c, t % CT, small[1])
                    if 0 <= r - LAG - 6 < 5 and exists(back(k, 2)):
                        finish_step(b, back(k, 2), r - LAG - 6)

            def layernorm(n, m, first_in, dst, done):
                def bc(s):
                    return s[:, :].unsqueeze(2).broadcast_to([P, T, F])
                v.tensor_tensor(X, X, first_in, ALU.add).then_inc(ln, 1)
                dve.wait_ge(ln, n + 1)
                v.tensor_reduce(mean[:, :], X, AX.X, ALU.add).then_inc(ln, 1)
                dve.wait_ge(ln, n + 2)
                v.tensor_scalar(mean[:, :], mean[:, :], 1.0 / F, None, ALU.mult).then_inc(ln, 1)
                dve.wait_ge(ln, n + 3)
                v.tensor_tensor(X, X, bc(mean), ALU.subtract).then_inc(ln, 1)
                dve.wait_ge(ln, n + 4)
                v.tensor_tensor(TMP, X, X, ALU.mult).then_inc(ln, 1)
                dve.wait_ge(ln, n + 5)
                v.tensor_reduce(var[:, :], TMP, AX.X, ALU.add).then_inc(ln, 1)
                dve.wait_ge(ln, n + 6)
                v.tensor_scalar(var[:, :], var[:, :], 1.0 / F, EPS, ALU.mult, ALU.add).then_inc(ln, 1)
                dve.wait_ge(std_done, m)
                v.reciprocal(rstd[:, :], std[:, :]).then_inc(ln, 1)
                dve.wait_ge(ln, n + 8)
                v.tensor_tensor(dst, X, bc(rstd), ALU.mult).then_inc(done, 1)

            def layer(b, l):
                n = b * LAYERS + l
                for g in range(NC):
                    q = slice(CT * g, CT * g + CT)
                    wxm = wx[g % 2][0:P, :].rearrange("p (t c) -> p t c", t=CT)[:, :, F:2 * F]
                    dve.wait_ge(self_done, n * NC + g + 1)
                    if g >= 1:
                        dve.wait_ge(m3_done, n * NC + g)
                    v.tensor_tensor(TMP[:, q, :], wxm, M3[:, q, 0:F], ALU.subtract).then_inc(m3_step, 1)
                    dve.wait_ge(m3_step, (n * NC + g) * 2 + 1)
                    v.tensor_copy(M3[:, q, F:2 * F], TMP[:, q, :]).then_inc(m3_step, 1)
                    dve.wait_ge(m3_step, (n * NC + g) * 2 + 2)
                    v.tensor_tensor(M3[:, q, 2 * F:3 * F], TMP[:, q, :], M3[:, q, F:2 * F], ALU.subtract
                                    ).then_inc(m3_done, 1)
                for q in range(T // 2):
                    m = n * (T // 2) + q + 1
                    dve.wait_ge(acc_full, m)
                    v.tensor_reduce(TMP[:, 2 * q:2 * q + 2, :],
                                    pAcc[0:P, q % 4, 0:6 * F].rearrange("p (t a f) -> p t f a", t=2, a=3),
                                    AX.X, ALU.add).then_inc(acc_done, 1)
                    dve.wait_ge(acc_done, m)
                    v.tensor_tensor(HC[:, 2 * q:2 * q + 2, :], TMP[:, 2 * q:2 * q + 2, :],
                                    SELF[:, 2 * q:2 * q + 2, :], ALU.add).then_inc(add_done, 1)
                dve.wait_ge(add_done, (n + 1) * (T // 2))
                v.tensor_scalar(HC, HC, floor[:, bass.ds(l, 1)], None, ALU.max).then_inc(hc_ready, 1)

            with dve.Fori(0, B) as b:
                prologue(b)
                body(b, 0)
                body(b, 1)
                with dve.Fori(2, NC) as k:
                    body(b, (k, 0))
                body(b, NC)
                body(b, NC + 1, LAG + 11)
                dve.wait_ge(x_res, (b + 1) * 16)
                dve.wait_ge(fin, (b + 1) * (5 * NC))
                layernorm(b * 16, b * 2 + 1, H0[:, :, :], HC, hc_ready)
                with dve.Fori(0, LAYERS) as l:
                    layer(b, l)
                dve.wait_ge(x1_done, b + 1)
                dve.wait_ge(hc_ready, (b + 1) * (LAYERS + 1))
                layernorm(b * 16 + 8, b * 2 + 2, HC, HC, y_done)

        @block.scalar
        def _(act):
            cp = nc.scalar.copy
            act.wait_ge(consts, N_CONST)
            act.wait_ge(w_turned, 1)
            cp(W3[0:F, :, :], pA[0:F, 0, 0:2 * F * LAYERS].rearrange("p (l c) -> p l c", l=LAYERS)
               ).then_inc(w_placed, 1)

            def prologue(b):
                for c in range(NC + 1):
                    if c < NC:
                        act.wait_ge(x_turned, upto(b, c, 1, 1))
                        if c >= 2:
                            act.wait_ge(val_full, upto(b, c, 1, -1))
                        cp(xT[:, c % 2, :], pA[0:F, c % 2, 0:C]).then_inc(x_sb, 1)
                    if c >= 1:
                        d = c - 1
                        act.wait_ge(proj_full, upto(b, d, 1, 1))
                        if d >= 2:
                            act.wait_ge(scr_out[d % 2], (b * (NC // 2) + d // 2) * 16)
                        cp(parts[:, d % 2, 0, :], pB[:, 0, d % 2, 0:C]).then_inc(high_done, 1)
                        act.wait_ge(val_full, upto(b, d, 1, 1))
                        cp(VA[:, CT * d:CT * d + CT, :, 0:D],
                           pB[0:P, 1, d % 2, 0:CT * F].rearrange("p (t h d) -> p t h d", t=CT, h=H)
                           ).then_inc(val_done, 1)

            def empty(b, k, n):
                _, kind, i, ago = plan_of(k)[n]
                c = back(k, ago)
                act.wait_ge(turned[kind], nth(b, c, kind, i))
                if kind == "mask":
                    t, j = i // NJ, i % NJ
                    cp(MT[:, slot(c, 2), BPP * j:BPP * j + BPP, P * t:P * t + P], misc16[0:P, :, 0:P]
                       ).then_inc(placed[kind], 1)
                elif kind == "shift":
                    cp(FQ[KS:KX, slot(c, 2), :, P * i:P * i + P], misc16[KS:KX, 0:H, 0:P]).then_inc(placed[kind], 1)
                else:
                    cp(ON[:, :, :, :], misc[0:P, :].rearrange("p (t h v) -> p t h v", t=CT, h=H)[:, :, :, 0:V]
                       ).then_inc(placed[kind], 1)

            def exp_b(b, k, u):
                act.wait_ge(sx_full, upto(b, k, UNITS, u + 1))
                if u >= 4 or not (isinstance(k, int) and k == 0):
                    act.wait_ge(pv_done, upto(b, k, T, u // 2 - 1))
                nc.scalar.activation(banks(E[0:P, u % 4, :]), bank_b(k, u)[0:P, :, 0:C], ACT.Exp, scale=0.2
                                     ).then_inc(exp_done, 1)

            def body(b, k, steps=UNITS):
                plan = plan_of(k)
                n = 0
                for r in range(steps):
                    c, u = unit_b(k, r - LAG - 1)
                    if c is not None:
                        exp_b(b, c, u)
                    if r == LAG + 4 and exists(back(k, 2)):
                        act.wait_ge(pv_done, upto(b, back(k, 1), T, 0))
                        cp(OT[:, :], pO[:, 0:C]).then_inc(ot_done, 1)
                    while n < len(plan) and plan[n][0] <= r:
                        empty(b, k, n)
                        n += 1

            def root(n, m):
                act.wait_ge(ln, n + 7)
                nc.scalar.activation(std[:, :], var[:, :], ACT.Sqrt).then_inc(std_done, 1)

            def layer(b, l):
                n = b * LAYERS + l
                for g in range(NC + 1):
                    if g < NC:
                        act.wait_ge(ht_full, n * NC + g + 1)
                        cp(HT[0:F, C * g:C * g + C], pA[0:F, g % 2, 0:C]).then_inc(ht_done, 1)
                    if g >= 1:
                        d = g - 1
                        q = slice(CT * d, CT * d + CT)
                        w = wx[d % 2][0:P, :].rearrange("p (t c) -> p t c", t=CT)
                        act.wait_ge(wx_full, n * NC + d + 1)
                        cp(M3[:, q, 0:F], w[:, :, F:2 * F])
                        cp(SELF[:, q, :], w[:, :, 0:F]).then_inc(self_done, 1)

            with act.Fori(0, B) as b:
                prologue(b)
                body(b, 0)
                body(b, 1)
                with act.Fori(2, NC) as k:
                    body(b, (k, 0))
                body(b, NC)
                body(b, NC + 1, LAG + 6)
                root(b * 16, 0)
                act.wait_ge(hc_ready, b * (LAYERS + 1) + 1)
                cp(X, HC).then_inc(x1_done, 1)
                with act.Fori(0, LAYERS) as l:
                    layer(b, l)
                root(b * 16 + 8, 1)

        @block.gpsimd
        def _(pool):
            g = nc.gpsimd
            g.memset(ident[:, :], 0.0).then_inc(ident_step, 1)
            pool.wait_ge(ident_step, 1)
            g.affine_select(out=ident[:, :], in_=ident[:, :], compare_op=ALU.not_equal, fill=1.0, base=0,
                            pattern=[[-1, 128]], channel_multiplier=1).then_inc(ident_step, 1)
            pool.wait_ge(ident_step, 2)
            g.tensor_copy(ident16[:, :], ident[:, :]).then_inc(ident_step, 1)

            def quarter(b, k):
                pool.wait_ge(fs_in, upto(b, k, 96, 96))
                if k >= 2:
                    pool.wait_ge(sx_full, upto(b, back(k, 1), UNITS, 0))
                apart(pool)
                g.tensor_scalar(FQ[0:KS, slot(k, 2), :, :], FS[:, slot(k, 3), :, :], 0.25, 1.0, ALU.mult, ALU.mult
                                ).then_inc(fq_ready, 1)

            def mask(b, k, p):
                pool.wait_ge(a_in[p % 2], upto(b, k, 8 * PIECES, (p // 2 + 1) * 16))
                if p >= 3:
                    pool.wait_ge(max_done, upto(b, k, UNITS, (p - 2) * H + 1))
                    pool.wait_ge(turned["mask"], nth(b, k, "mask", p - 3))
                elif k >= 1:
                    pool.wait_ge(max_done, upto(b, back(k, 1), UNITS, (p - 2 + PIECES) * H + 1))
                    pool.wait_ge(turned["mask"], nth(b, k, "mask", p - 3))
                apart(pool)
                g.tensor_scalar(M16[:, p % 3, :], A32[:, p % 2, :], -1.0, BIG, ALU.add, ALU.mult
                                ).then_inc(m16_ready, 1)

            def adjacency8(b, k, t):
                pool.wait_ge(placed["mask"], nth(b, k, "mask", NJ * t + NJ - 1))
                q = C * k + P * t
                apart(pool)
                g.tensor_scalar(AT[:, :, q:q + P], MT[:, slot(k, 2), :, P * t:P * t + P], ONE8 / BIG, ONE8,
                                ALU.mult, ALU.add).then_inc(at_done, 1)

            with pool.Fori(0, B) as b:
                for k in range(NC):
                    for p in range(PIECES):
                        mask(b, k, p)
                        if p == 4:
                            quarter(b, k)
                        if p % NJ == NJ - 1 and p >= 2 * NJ - 1:
                            adjacency8(b, k, p // NJ - 1)
                    adjacency8(b, k, CT - 1)


_INS = ["x", "adj", "L0_gnn_kernel", "L0_gnn_attention_kernel", "L0_gnn_attention_kernel_2", "L0_gnn_bias",
        "L1_gnn_Wm0", "L1_gnn_Ws0", "L1_gnn_b0", "L1_gnn_Wm1", "L1_gnn_Ws1", "L1_gnn_b1",
        "L1_gnn_Wm2", "L1_gnn_Ws2", "L1_gnn_b2"]


def kernel(**inputs):
    import concourse.bacc as bacc
    import numpy as np
    from concourse.bass_utils import run_bass_kernel_spmd

    nc = bacc.Bacc("TRN2", target_bir_lowering=False, num_devices=1, dynamic_dma_scratch_size=1024)
    arrays, args = {}, {}
    for name in _INS:
        a = np.ascontiguousarray(inputs[name])
        arrays[f"in_{name}"] = a
        args[name] = nc.dram_tensor(f"in_{name}", a.shape, mybir.dt.from_np(a.dtype), kind="ExternalInput").ap()
    out = nc.dram_tensor("out_0", (B, N, F), F32, kind="ExternalOutput").ap()
    build(nc, args["x"], args["adj"], args["L0_gnn_kernel"], args["L0_gnn_attention_kernel"],
          args["L0_gnn_attention_kernel_2"], args["L0_gnn_bias"],
          [args[f"L1_gnn_Wm{l}"] for l in range(LAYERS)], [args[f"L1_gnn_Ws{l}"] for l in range(LAYERS)],
          [args[f"L1_gnn_b{l}"] for l in range(LAYERS)], out)
    r = run_bass_kernel_spmd(nc, [arrays], core_ids=[0])
    return r.results[0]["out_0"]
```

```python
from contextlib import ExitStack

import concourse.bass as bass
from concourse import mybir

F32 = mybir.dt.float32
BF16 = mybir.dt.bfloat16
FP8 = mybir.dt.float8e4
U8 = mybir.dt.uint8
ALU = mybir.AluOpType
ACT = mybir.ActivationFunctionType
AX = mybir.AxisListType

B, N, F = 8, 3000, 64
H, D = 4, 16
HD = H * D
P = 125
T = N // P
CT = 4
C = CT * P
NC = N // C
PIECE = 2 * C
NJ = N // PIECE
BPP = PIECE // P
LAYERS = 3
PAIRS = H // 2
KS = 6 * D
KX = KS + 2
V = D + 1
UNITS = CT * NJ * H
assert UNITS == T * PAIRS == T // 2 * 4
PIECES = CT * NJ
GROUPS = 3
GROUP_UNITS = UNITS // GROUPS
LAG = 5
BIG = 2.0 ** 35
ONE8 = 56.0
EPS = 1e-5
NEG = -3.0e38
PART_S = (0, 0, 1, 1, 0, 2)
PART_O = (0, 1, 0, 1, 2, 0)


def turn_plan():
    plan = [(4 * p + 1, "mask", p, 0) for p in range(PIECES)]
    for t in range(CT):
        step = (t + 1) * NJ * H + 4
        plan.append((step % UNITS, "shift", t, step // UNITS))
    plan.append((LAG + 5, "result", 0, 2))
    return sorted(plan)


PLAN = turn_plan()
assert PLAN[-1][1:] == ("mask", PIECES - 1, 0)


def back(k, n):
    return k - n if isinstance(k, int) else (k[0], k[1] - n)


def exists(k):
    return not isinstance(k, int) or 0 <= k < NC


def slot(k, n):
    return k % n if isinstance(k, int) else (k[0] + k[1] % n) % n


def upto(b, k, per, i):
    if isinstance(k, int):
        return b * (NC * per) + (k * per + i)
    return (b * NC + k[0]) * per + (k[1] * per + i)


def upto_b(b, k, per, i):
    if isinstance(k, int):
        return (b * NC + k) * per + i
    return (b * NC + k[0]) * per + (k[1] * per + i)


def first_tile(k):
    return k * CT if isinstance(k, int) else k[0] * CT + k[1] * CT


def plan_of(k):
    return [t for t in PLAN if exists(back(k, t[3]))]


def unit_b(k, x):
    c, u = (back(k, 1), x) if x >= 0 else (back(k, 2), x + UNITS)
    return (c, u) if exists(c) else (None, -1)


def build(nc, x, adj, kernel, att1, att2, bias, wm, ws, bb, out):
    scratch = nc.dram_tensor("scratch", (3, 2 * HD, N), BF16, kind="Internal").ap()

    with ExitStack() as ctx:
        def sb(name, shape, dt):
            return ctx.enter_context(nc.sbuf_tensor(name, shape, dt))

        def psum(name, shape, dt):
            return ctx.enter_context(nc.psum_tensor(name, shape, dt))

        def sem(name):
            return ctx.enter_context(nc.semaphore(name))

        AT = sb("AT", [P, T, N], U8)
        MT = sb("MT", [P, 2, T, C], BF16)
        FO = sb("FO", [KX, H, N], BF16)
        FS = sb("FS", [KS, 3, H, C], BF16)
        FQ = sb("FQ", [KX, 2, H, C], BF16)
        A32 = sb("A32", [P, 2, PIECE], F32)
        M16 = sb("M16", [P, 3, PIECE], BF16)
        E = sb("E", [128, 4, PIECE], F32)
        VA = sb("VA", [P, T, H, V], F32)
        OT = sb("OT", [128, C], F32)
        ON = sb("ON", [P, CT, H, V], F32)
        H0 = sb("H0", [P, T, HD], F32)
        ident = sb("ident", [128, 128], F32)
        ident16 = sb("ident16", [128, 128], BF16)
        cm = sb("cm", [P, 2, H, NJ], F32)
        mx = sb("mx", [P, H], F32)
        sh = sb("sh", [P, H], F32)
        sh2 = sb("sh2", [P, H], F32)
        shift = sb("shift", [P, H, 2], BF16)
        den = sb("den", [P, CT, H], F32)
        rden = sb("rden", [P, CT, H], F32)
        wqk = sb("wqk", [F, 2 * HD], F32)
        wv = sb("wv", [F, HD], F32)
        biasb = sb("biasb", [P, HD], F32)
        HT = sb("HT", [F + 1, N], F32)
        W3 = sb("W3", [F + 1, LAYERS, 2 * F], F32)
        mean = sb("mean", [P, T], F32)
        var = sb("var", [P, T], F32)
        std = sb("std", [P, T], F32)
        rstd = sb("rstd", [P, T], F32)

        work = MT[:, 1, :, :].rearrange("p t c -> p (t c)").bitcast(F32)
        TF = T * F
        TH = T // 2
        X = work[:, 0:TF].rearrange("p (t f) -> p t f", f=F)
        HC = work[:, TF:2 * TF].rearrange("p (t f) -> p t f", f=F)
        SELF = work[:, 2 * TF:3 * TF].rearrange("p (t f) -> p t f", f=F)
        M3A = work[:, 3 * TF:3 * TF + TH * 3 * F // 2].bitcast(BF16).rearrange("p (t c) -> p t c", c=3 * F)
        assert 3 * TF + TH * 3 * F // 2 <= T * C // 2
        TMP = H0[:, :, :]
        free = E[:, :, :].rearrange("p s c -> p (s c)")
        at = TH * 3 * F // 2
        M3B = free[0:P, 0:at].bitcast(BF16).rearrange("p (t c) -> p t c", c=3 * F)
        xin = free[0:P, at:at + CT * F].rearrange("p (t f) -> p t f", f=F)
        at += CT * F
        xT = free[0:F, at:at + C]
        at += C
        rest = free[:, at:at + C]
        at += C
        parts = free[:, at:at + 3 * C // 2].bitcast(BF16).rearrange("p (a c) -> p a c", a=3)
        assert at + 3 * C // 2 <= 4 * PIECE and 2 * HD == 128

        def m3(tiles, cols):
            if isinstance(tiles, int):
                return M3A[:, tiles, cols] if tiles < TH else M3B[:, tiles - TH, cols]
            if tiles.stop <= TH:
                return M3A[:, tiles, cols]
            return M3B[:, tiles.start - TH:tiles.stop - TH, cols]

        pA = psum("pA", [128, 2, 512], F32)
        pB = psum("pB", [128, 2, 2, 512], F32)
        pO = psum("pO", [128, 512], F32)
        misc = psum("misc", [128, 512], F32)
        misc16 = misc[:, :].bitcast(BF16).rearrange("p (b c) -> p b c", c=128)
        pAcc = pB[:, 0, :, :]
        pX, pV, pP = pA[:, 0, :], pA[:, 1, :], misc
        wx = (pB[:, 1, 0, :], pB[:, 1, 1, :], pB[:, 0, 0, :], pB[:, 0, 1, :])
        assert NC <= 6

        w_loaded = sem("w_loaded")
        consts = sem("consts")
        ident_step = sem("ident_step")
        w_turned = sem("w_turned")
        w_placed = sem("w_placed")
        x_in = sem("x_in")
        x_turned = sem("x_turned")
        x_sb = sem("x_sb")
        proj_full = sem("proj_full")
        val_full = sem("val_full")
        high_done = sem("high_done")
        val_done = sem("val_done")
        rest_done = sem("rest_done")
        mid_done = sem("mid_done")
        parts_done = sem("parts_done")
        scr_out = sem("scr_out")
        fo_in = sem("fo_in")
        fs_in = sem("fs_in")
        a_in = [sem("a_in0"), sem("a_in1")]
        m16_ready = sem("m16_ready")
        fq_ready = sem("fq_ready")
        sn_full = sem("sn_full")
        max_done = sem("max_done")
        stat = sem("stat")
        shift_done = sem("shift_done")
        turned = {"mask": sem("mask_turned"), "shift": sem("shift_turned"), "result": sem("result_turned")}
        placed = {"mask": sem("mask_placed"), "shift": sem("shift_placed"), "result": sem("result_placed")}
        at_done = sem("at_done")
        sm_full = sem("sm_full")
        relu_done = sem("relu_done")
        sx_full = sem("sx_full")
        exp_done = sem("exp_done")
        pv_done = sem("pv_done")
        ot_done = sem("ot_done")
        fin = sem("fin")
        x_res = sem("x_res")
        ln1 = sem("ln1")
        ln2 = sem("ln2")
        std_done = sem("std_done")
        x1_done = sem("x1_done")
        hc_ready = sem("hc_ready")
        hc_part = sem("hc_part")
        ht_full = sem("ht_full")
        ht_done = sem("ht_done")
        wx_full = sem("wx_full")
        self_done = sem("self_done")
        m3_step = sem("m3_step")
        m3_done = sem("m3_done")
        acc_full = sem("acc_full")
        acc_done = sem("acc_done")
        add_done = sem("add_done")
        y_done = sem("y_done")
        y_out = sem("y_out")
        passed = sem("passed")

        x_v = x.rearrange("b (t p) f -> b p t f", p=P)
        out_v = out.rearrange("b (t p) f -> b p t f", p=P)
        adj_v = adj.rearrange("b (t p) (j c) -> b t j p c", p=P, c=PIECE)
        scr_v = scratch.rearrange("a p n -> p a n")
        id_p = ident[0:P, 0:P]
        id16 = ident16[0:P, 0:P]

        def banks(ap):
            return ap.rearrange("p (a c) -> p a c", a=2)

        def two_places(k, u):
            return isinstance(k, int) and (k == 0 or k == 1 and u <= LAG)

        def bank_a(k, u):
            return (pA[:, :, :], pB[:, 1, :, :])[u % 2 if two_places(k, u) else 0]

        def place_alone(k, u):
            if isinstance(k, int) and k >= NC - 2:
                return u + LAG - UNITS * (NC - 1 - k)
            return -1

        def bank_b(k, u):
            i = place_alone(k, u)
            return (pB[:, 1, :, :], pB[:, 0, :, :], pA[:, :, :])[i % 3] if i >= 0 else pB[:, u % 2, :, :]

        PER_CHUNK = {"mask": PIECES, "shift": CT, "result": 1}

        def nth(b, k, kind, i):
            return upto(b, k, PER_CHUNK[kind], i + 1)

        N_CONST = 6

        def apart(eng):
            eng.sem_inc(passed, 1)

        block = ctx.enter_context(nc.Block())

        @block.sync
        def _(sp):
            for dst, src in ((wqk[:, 0:HD], att1), (wqk[:, HD:2 * HD], att2), (wv[:, :], kernel)):
                sp.dma_start(dst.rearrange("f (h d) -> f h d", h=H), src.rearrange("h f d -> f h d")
                             ).then_inc(w_loaded, 16)
            sp.dma_start(biasb[:, :], bias.rearrange("a b h d -> (a b h d)").partition_broadcast(P)
                         ).then_inc(w_loaded, 16)
            for l in range(LAYERS):
                sp.dma_start(SELF[0:F, l, :], ws[l]).then_inc(w_loaded, 16)
                sp.dma_start(TMP[0:F, l, :], wm[l]).then_inc(w_loaded, 16)
            sp.wait_ge(consts, N_CONST)
            for l in range(LAYERS):
                sp.dma_start(W3[F:F + 1, l, 0:F], bb[l].unsqueeze(0)).then_inc(w_loaded, 16)

            def projections(b, run):
                for c in range(NC):
                    if c >= 1:
                        sp.wait_ge(x_turned, upto(run, c, 1, 0))
                        apart(sp)
                    sp.dma_start(xin, x_v[b, :, CT * c:CT * c + CT, :]).then_inc(x_in, 16)
                    if c >= 1:
                        store_parts(run, c - 1)
                store_parts(run, NC - 1)

            def store_parts(run, c):
                sp.wait_ge(parts_done, upto(run, c, 1, 1))
                apart(sp)
                sp.dma_start(scr_v[:, :, C * c:C * c + C], parts).then_inc(scr_out, 16)

            def load_queries(k, slot):
                for g in range(6):
                    sp.dma_start(FS[D * g:D * g + D, slot, :, :],
                                 scratch[PART_S[g], 0:HD, bass.ds(k * C, C)].rearrange(
                                     "(h d) n -> d h n", h=H)).then_inc(fs_in, 16)

            def load_rows(b, run, k):
                for p in range(PIECES):
                    sp.wait_ge(m16_ready, upto(run, k, PIECES, p + 1))
                    apart(sp)
                    sp.dma_start(A32[:, p % 2, :], adj_v[b, first_tile(k) + p // NJ, p % NJ]
                                 ).then_inc(a_in[p % 2], 16)

            def start_graph(b, run):
                projections(b, run)
                sp.wait_ge(scr_out, (run + 1) * (16 * NC))
                apart(sp)
                for g in range(6):
                    sp.dma_start(FO[D * g:D * g + D, :, :],
                                 scratch[PART_O[g], HD:2 * HD, :].rearrange("(h d) n -> d h n", h=H)
                                 ).then_inc(fo_in, 16)
                load_queries(0, 0)
                load_rows(b, run, 0)

            start_graph(0, 0)
            with sp.Fori(0, B) as b:
                load_queries(1, 1)
                load_rows(b, b, 1)
                load_queries(2, 2)
                with sp.Fori(2, NC - 1) as k:
                    load_rows(b, b, (k, 0))
                    sp.wait_ge(sm_full, upto(b, (k, -1), UNITS, 0))
                    apart(sp)
                    load_queries(k + 1, (k + 1) % 3)
                load_rows(b, b, NC - 1)
                sp.wait_ge(sx_full, (b + 1) * (NC * UNITS))
                apart(sp)
                sp.wait_ge(at_done, (b + 1) * T)
                apart(sp)
                sp.dma_start(X, x_v[b]).then_inc(x_res, 16)
                sp.wait_ge(pv_done, (b + 1) * (NC * T))
                apart(sp)
                start_graph((b + 1) % B, b + 1)

        @block.tensor
        def _(pe):
            mm = nc.tensor.matmul

            pe.wait_ge(ident_step, 3)
            pe.wait_ge(w_loaded, 16 * (4 + 3 * LAYERS))
            for l in range(LAYERS):
                for o, w in ((0, SELF), (F, TMP)):
                    last = nc.tensor.transpose(pA[0:F, 0, 2 * F * l + o:2 * F * l + o + F], w[0:F, l, :],
                                               ident[0:F, 0:F])
            last.then_inc(w_turned, 1)
            pe.wait_ge(w_placed, 1)

            def turn_x(n):
                pe.wait_ge(x_in, n * 16 + 16)
                apart(pe)
                for t in range(CT):
                    last = nc.tensor.transpose(pX[0:F, P * t:P * t + P], xin[:, t, :], id_p)
                last.then_inc(x_turned, 1)

            def project(n):
                pe.wait_ge(x_sb, n + 1)
                if not (isinstance(n, int) and n == 0):
                    pe.wait_ge(rest_done, n)
                mm(pP[:, 0:C], wqk[:, :], xT, start=True, stop=True).then_inc(proj_full, 1)

            def project_values(n):
                if not (isinstance(n, int) and n == 0):
                    pe.wait_ge(val_done, n)
                for t in range(CT):
                    last = mm(pV[0:P, F * t:F * t + F], xT[:, P * t:P * t + P], wv[:, :],
                              start=True, stop=True)
                last.then_inc(val_full, 1)

            def scores_a(b, k, u):
                t, j, h = u // (NJ * H), u // H % NJ, u % H
                if u == 0:
                    pe.wait_ge(fs_in, upto(b, k, 96, 96))
                if not two_places(k, u):
                    pe.wait_ge(max_done, upto(b, k, UNITS, u + 1))
                elif k == 1 or u >= 2:
                    pe.wait_ge(max_done, upto(b, k, UNITS, u))
                elif u == 0:
                    pe.wait_ge(fo_in, (b + 1) * 96)
                for a in range(2):
                    last = mm(bank_a(k, u)[0:P, a, 0:C], FS[:, slot(k, 3), h, P * t:P * t + P],
                              FO[0:KS, h, PIECE * j + C * a:PIECE * j + C * a + C], start=True, stop=True)
                last.then_inc(sn_full, 1)

            def turn(b, k, n):
                plan = plan_of(k)
                _, kind, i, ago = plan[n]
                if n > 0:
                    _, before, j, c = plan[n - 1]
                    pe.wait_ge(placed[before], nth(b, back(k, c), before, j))
                elif not (isinstance(k, int) and k == 0):
                    _, before, j, c = plan_of(back(k, 1))[-1]
                    pe.wait_ge(placed[before], nth(b, back(k, 1 + c), before, j))
                if kind == "mask":
                    pe.wait_ge(m16_ready, upto(b, k, PIECES, i + 3))
                    for s in range(BPP):
                        last = nc.tensor.transpose(misc16[0:P, s, 0:P], M16[:, i % 3, P * s:P * s + P], id16)
                elif kind == "shift":
                    pe.wait_ge(shift_done, nth(b, back(k, ago), "shift", i))
                    for h in range(H):
                        last = nc.tensor.transpose(misc16[KS:KX, h, 0:P], shift[:, h, :], id16)
                else:
                    pe.wait_ge(ot_done, nth(b, back(k, ago), "result", i))
                    apart(pe)
                    for t in range(CT):
                        last = nc.tensor.transpose(misc[0:P, 128 * t:128 * t + 128], OT[:, P * t:P * t + P],
                                                   ident[:, :])
                last.then_inc(turned[kind], 1)

            def scores_b(b, k, u):
                i, pair = u // PAIRS, u % PAIRS
                place = place_alone(k, u)
                if place < 2:
                    pe.wait_ge(exp_done, upto_b(b, k, UNITS, u + 1))
                elif place == 2:
                    pe.wait_ge(max_done, upto(b, NC, UNITS, 1))
                else:
                    pe.wait_ge(exp_done, upto_b(b, k, UNITS, u))
                for a in range(2):
                    h = 2 * pair + a
                    last = mm(bank_b(k, u)[0:P, a, 0:C], FO[0:KS, h, P * i:P * i + P], FS[:, slot(k, 3), h, :],
                              start=True, stop=True)
                last.then_inc(sm_full, 1)

            def exponent_b(b, k, u):
                i, pair = u // PAIRS, u % PAIRS
                if u == 0:
                    pe.wait_ge(fq_ready, upto(b, k, 1, 1))
                    pe.wait_ge(placed["shift"], nth(b, k, "shift", CT - 1))
                pe.wait_ge(relu_done, upto_b(b, k, UNITS, u + 1))
                for a in range(2):
                    h = 2 * pair + a
                    last = mm(bank_b(k, u)[0:P, a, 0:C], FO[0:KX, h, P * i:P * i + P], FQ[:, slot(k, 2), h, :],
                              start=False, stop=True, skip_group_check=True)
                last.then_inc(sx_full, 1)

            def values_b(b, k, i):
                pe.wait_ge(exp_done, upto_b(b, k, UNITS, 2 * i + 4))
                if i == 0 and not (isinstance(k, int) and k == 0):
                    pe.wait_ge(ot_done, upto(b, k, 1, 0))
                for h in range(H):
                    last = mm(pO[32 * h:32 * h + V, 0:C], VA[:, i, h, :],
                              E[0:P, (2 * i + h // 2) % 4, C * (h % 2):C * (h % 2) + C],
                              start=(i == 0), stop=(i == T - 1))
                last.then_inc(pv_done, 1)

            def step(b, k, r):
                c, u = unit_b(k, r - LAG - 2)
                if c is not None:
                    exponent_b(b, c, u)
                v, w = unit_b(k, r - LAG - 5)
                values = v is not None and w % 2 == 0
                alone = not exists(k)
                if values and not alone:
                    values_b(b, v, w // 2)
                if exists(k) and r < UNITS:
                    scores_a(b, k, r)
                for n, at in enumerate(plan_of(k)):
                    if at[0] == r:
                        turn(b, k, n)
                c, u = unit_b(k, r - LAG)
                if c is not None:
                    scores_b(b, c, u)
                if values and alone:
                    values_b(b, v, w // 2)

            def body(b, k, steps=UNITS):
                for r in range(steps):
                    step(b, k, r)

            def layer(b, l):
                n = b * LAYERS + l
                last_layer = isinstance(l, int)
                pe.wait_ge(hc_ready, b * LAYERS + l + 1)
                for g in range(NC + 1):
                    if g < NC:
                        if g >= 2:
                            pe.wait_ge(ht_done, n * NC + g - 1)
                        apart(pe)
                        for t in range(CT):
                            last = nc.tensor.transpose(pA[0:F, g % 2, P * t:P * t + P], HC[:, CT * g + t, :],
                                                       id_p)
                        last.then_inc(ht_full, 1)
                    if g >= 1:
                        d = g - 1
                        pe.wait_ge(ht_done, n * NC + d + 1)
                        if d >= 4:
                            pe.wait_ge(m3_done, n * NC + d - 3)
                        for t in range(CT):
                            q = C * d + P * t
                            last = mm(wx[d % 4][0:P, 2 * F * t:2 * F * t + 2 * F], HT[:, q:q + P],
                                      W3[:, l, :], start=True, stop=True)
                        last.then_inc(wx_full, 1)
                for t in range(T):
                    c = b * NC + l * (NC // 2) + (NC + t // 8)
                    if not last_layer and t % 8 == 0:
                        turn_x(c)
                    if not last_layer and t % 8 == 2:
                        project(c)
                    if not last_layer and t % 8 == 4:
                        project_values(c)
                    if t % 2 == 0 and t >= 4:
                        pe.wait_ge(acc_done, n * (T // 2) + t // 2 - 1)
                        apart(pe)
                    for i in range(T):
                        if t == 0 and i in (0, TH):
                            pe.wait_ge(m3_done, n * NC + (NC if i else NC // 2))
                            apart(pe)
                        if last_layer and (t * T + i) % (T * T // UNITS) == 0:
                            step(b + 1, 0, (t * T + i) // (T * T // UNITS))
                            apart(pe)
                        last = mm(pAcc[0:P, t // 2 % 2, 3 * F * (t % 2):3 * F * (t % 2) + 3 * F],
                                  AT[:, i, P * t:P * t + P].bitcast(FP8), m3(i, slice(0, 3 * F)),
                                  start=(i == 0), stop=(i == T - 1))
                    if t % 2:
                        last.then_inc(acc_full, 1)
                if not last_layer:
                    pe.wait_ge(rest_done, b * NC + l * (NC // 2) + (NC + NC // 2))
                    pe.wait_ge(val_done, b * NC + l * (NC // 2) + (NC + NC // 2))

            for c in range(NC):
                turn_x(c)
                project(c)
                project_values(c)
            pe.wait_ge(rest_done, NC)
            pe.wait_ge(val_done, NC)
            body(0, 0)
            with pe.Fori(0, B) as b:
                body(b, 1)
                with pe.Fori(2, NC) as k:
                    body(b, (k, 0))
                body(b, NC)
                body(b, NC + 1, LAG + 6)
                with pe.Fori(0, LAYERS - 1) as l:
                    layer(b, l)
                layer(b, LAYERS - 1)
                pe.wait_ge(acc_done, (b + 1) * (LAYERS * (T // 2)))

        @block.vector
        def _(dve):
            v = nc.vector
            v.memset(FO[KS:KX, :, :], 1.0).then_inc(consts, 1)
            v.memset(VA[:, :, :, :], 1.0).then_inc(consts, 1)
            v.memset(OT[:, :], 0.0).then_inc(consts, 1)
            v.memset(pO[:, :], 0.0).then_inc(consts, 1)
            v.memset(W3[:, :, :], 0.0).then_inc(consts, 1)
            v.memset(HT[F:F + 1, :], 1.0).then_inc(consts, 1)
            dve.sem_inc(max_done, 1)
            dve.sem_inc(y_out, 16)
            dve.sem_inc(exp_done, 2)
            dve.sem_inc(m16_ready, 2)
            dve.wait_ge(consts, N_CONST)

            def split(n):
                dve.wait_ge(high_done, n + 1)
                if not (isinstance(n, int) and n == 0):
                    dve.wait_ge(parts_done, n)
                v.tensor_tensor(rest, pP[:, 0:C], parts[:, 0, :], ALU.subtract).then_inc(rest_done, 1)
                dve.wait_ge(rest_done, n + 1)
                v.tensor_copy(parts[:, 1, :], rest).then_inc(mid_done, 1)
                dve.wait_ge(mid_done, n + 1)
                v.tensor_tensor(parts[:, 2, :], rest, parts[:, 1, :], ALU.subtract).then_inc(parts_done, 1)

            def maximum_a(b, k, u):
                p, h = u // H, u % H
                if h == 0:
                    dve.wait_ge(m16_ready, upto(b, k, PIECES, p + 3))
                dve.wait_ge(sn_full, upto(b, k, UNITS, u + 1))
                apart(dve)
                pu = bank_a(k, u)[0:P, :, 0:C]
                v.tensor_tensor_reduce(pu, pu, banks(M16[:, p % 3, :]), 1.0, NEG,
                                       ALU.add, ALU.max, cm[:, p // NJ % 2, h, p % NJ:p % NJ + 1]).then_inc(max_done, 1)

            def shift_step(b, k, t, i):
                n = nth(b, k, "shift", t) * 4 - 4
                if i == 0:
                    dve.wait_ge(max_done, upto(b, k, UNITS, (t + 1) * NJ * H + 1))
                    v.tensor_reduce(mx[:, :], cm[:, t % 2, :, :], AX.X, ALU.max).then_inc(stat, 1)
                else:
                    dve.wait_ge(stat, n + i)
                if i == 1:
                    v.tensor_scalar(sh2[:, :], mx[:, :], -1.25, None, ALU.mult).then_inc(stat, 1)
                if i == 2:
                    v.scalar_tensor_tensor(out=sh[:, :], in0=mx[:, :], scalar=-0.25, op0=ALU.mult,
                                           in1=sh2[:, :], op1=ALU.min).then_inc(stat, 1)
                if i == 3:
                    v.tensor_copy(shift[:, :, 0], sh[:, :]).then_inc(stat, 1)
                if i == 4:
                    v.tensor_tensor(shift[:, :, 1], sh[:, :], shift[:, :, 0], ALU.subtract
                                    ).then_inc(shift_done, 1)

            def relu_b(b, k, u):
                if u == 0:
                    dve.wait_ge(placed["mask"], nth(b, k, "mask", PIECES - 1))
                dve.wait_ge(sm_full, upto(b, k, UNITS, u + 1))
                i = u // PAIRS
                pu = bank_b(k, u)[0:P, :, 0:C]
                v.scalar_tensor_tensor(out=pu, in0=pu, scalar=0.0, op0=ALU.max,
                                       in1=MT[:, slot(k, 2), i, :].unsqueeze(1).broadcast_to([P, 2, C]),
                                       op1=ALU.add).then_inc(relu_done, 1)

            def finish_step(b, k, i):
                h0 = H0[:, bass.ds(first_tile(k), CT), :]
                h04 = h0.rearrange("p t (h d) -> p t h d", h=H)
                if i == 0:
                    dve.wait_ge(placed["result"], nth(b, k, "result", 0))
                    v.tensor_scalar(den[:, :, :], ON[:, :, :, D], 1e-30, None, ALU.max).then_inc(fin, 1)
                else:
                    dve.wait_ge(fin, upto(b, k, 5, i))
                if i == 1:
                    v.reciprocal(rden[:, :, :], den[:, :, :]).then_inc(fin, 1)
                if i == 2:
                    v.tensor_tensor(h04, ON[:, :, :, 0:D],
                                    rden[:, :, :].unsqueeze(3).broadcast_to([P, CT, H, D]),
                                    ALU.mult).then_inc(fin, 1)
                if i == 3:
                    v.tensor_tensor(h0, h0, biasb[:, :].unsqueeze(1).broadcast_to([P, CT, HD]), ALU.add
                                    ).then_inc(fin, 1)
                if i == 4:
                    v.tensor_scalar(h0, h0, 0.0, None, ALU.max).then_inc(fin, 1)

            def step(b, k, r):
                since, t = (r + 1) % (NJ * H), (r + 1) // (NJ * H) - 1
                c = k if t >= 0 else back(k, 1)
                small = [2 * since - 1, 2 * since] if since <= 2 and exists(c) and r < UNITS else []
                if exists(k) and r < UNITS:
                    maximum_a(b, k, r)
                if small and small[0] >= 1:
                    shift_step(b, c, t % CT, small[0])
                c2, u = unit_b(k, r - LAG)
                if c2 is not None:
                    relu_b(b, c2, u)
                if small:
                    shift_step(b, c, t % CT, small[1])
                if 0 <= r - LAG - 6 < 5 and exists(back(k, 2)):
                    finish_step(b, back(k, 2), r - LAG - 6)

            def body(b, k, steps=UNITS):
                for r in range(steps):
                    step(b, k, r)

            def layernorm_step(i, q, n, m, sem, first_in, dst, done):
                xq = X[:, q, :]
                shape = [P, q.stop - q.start, F]

                def bc(s):
                    return s[:, q].unsqueeze(2).broadcast_to(shape)
                if i == 7:
                    dve.wait_ge(std_done, m)
                elif i > 0:
                    dve.wait_ge(sem, n + i)
                if i == 0:
                    v.tensor_tensor(xq, xq, first_in[:, q, :], ALU.add).then_inc(sem, 1)
                if i == 1:
                    v.tensor_reduce(mean[:, q], xq, AX.X, ALU.add).then_inc(sem, 1)
                if i == 2:
                    v.tensor_scalar(mean[:, q], mean[:, q], 1.0 / F, None, ALU.mult).then_inc(sem, 1)
                if i == 3:
                    v.tensor_tensor(xq, xq, bc(mean), ALU.subtract).then_inc(sem, 1)
                if i == 4:
                    v.tensor_tensor(TMP[:, q, :], xq, xq, ALU.mult).then_inc(sem, 1)
                if i == 5:
                    v.tensor_reduce(var[:, q], TMP[:, q, :], AX.X, ALU.add).then_inc(sem, 1)
                if i == 6:
                    v.tensor_scalar(var[:, q], var[:, q], 1.0 / F, EPS, ALU.mult, ALU.add).then_inc(sem, 1)
                if i == 7:
                    v.reciprocal(rstd[:, q], std[:, q]).then_inc(sem, 1)
                if i == 8:
                    v.tensor_tensor(dst[:, q, :], xq, bc(rstd), ALU.mult).then_inc(done, 1)

            def second_layernorm(b, g, i):
                if i == 0:
                    dve.wait_ge(x1_done, b + 1)
                    dve.wait_ge(add_done, (b * LAYERS + LAYERS - 1) * (T // 2) + (g + 1) * (T // 2 // GROUPS))
                size = T // GROUPS
                layernorm_step(i, slice(g * size, (g + 1) * size), b * (8 * GROUPS) + 8 * g,
                               b * (GROUPS + 1) + g + 2, ln2, HC, TMP, y_done)

            def layer(b, l):
                n = b * LAYERS + l
                for g in range(NC):
                    q = slice(CT * g, CT * g + CT)
                    wxm = wx[g % 4][0:P, :].rearrange("p (t c) -> p t c", t=CT)[:, :, F:2 * F]
                    dve.wait_ge(self_done, n * NC + g + 1)
                    if g >= 1:
                        dve.wait_ge(m3_done, n * NC + g)
                    v.tensor_tensor(TMP[:, q, :], wxm, m3(q, slice(0, F)), ALU.subtract).then_inc(m3_step, 1)
                    dve.wait_ge(m3_step, (n * NC + g) * 2 + 1)
                    v.tensor_copy(m3(q, slice(F, 2 * F)), TMP[:, q, :]).then_inc(m3_step, 1)
                    dve.wait_ge(m3_step, (n * NC + g) * 2 + 2)
                    v.tensor_tensor(m3(q, slice(2 * F, 3 * F)), TMP[:, q, :], m3(q, slice(F, 2 * F)), ALU.subtract
                                    ).then_inc(m3_done, 1)
                for q in range(T // 2):
                    m = n * (T // 2) + q + 1
                    if isinstance(l, int):
                        for r in range(4 * q, 4 * q + 4):
                            step(b + 1, 0, r)
                            g, i = r // GROUP_UNITS - 1, r % GROUP_UNITS
                            if g >= 0 and i <= 6:
                                second_layernorm(b, g, i)
                            if g >= 0 and i in (10, 11):
                                second_layernorm(b, g, i - 3)
                    dve.wait_ge(acc_full, m)
                    v.tensor_reduce(TMP[:, 2 * q:2 * q + 2, :],
                                    pAcc[0:P, q % 2, 0:6 * F].rearrange("p (t a f) -> p t f a", t=2, a=3),
                                    AX.X, ALU.add).then_inc(acc_done, 1)
                    dve.wait_ge(acc_done, m)
                    v.tensor_tensor(HC[:, 2 * q:2 * q + 2, :], TMP[:, 2 * q:2 * q + 2, :],
                                    SELF[:, 2 * q:2 * q + 2, :], ALU.add).then_inc(add_done, 1)
                    if not isinstance(l, int) and q % 4 == 3:
                        dve.wait_ge(add_done, m)
                        eight = HC[:, 2 * q - 6:2 * q + 2, :]
                        v.tensor_scalar(eight, eight, 0.0, None, ALU.max
                                        ).then_inc(hc_ready if q == T // 2 - 1 else hc_part, 1)
                    if not isinstance(l, int) and q % 4 == 2:
                        split(b * NC + l * (NC // 2) + (NC + q // 4))

            for c in range(NC):
                split(c)
            body(0, 0)
            with dve.Fori(0, B) as b:
                body(b, 1)
                dve.wait_ge(y_out, (b + 1) * 16)
                apart(dve)
                with dve.Fori(2, NC) as k:
                    body(b, (k, 0))
                body(b, NC)
                body(b, NC + 1, LAG + 11)
                dve.wait_ge(x_res, (b + 1) * 16)
                dve.wait_ge(fin, (b + 1) * (5 * NC))
                for i in range(9):
                    layernorm_step(i, slice(0, T), b * 8, b * (GROUPS + 1) + 1, ln1, H0, HC, hc_ready)
                dve.wait_ge(hc_ready, b * LAYERS + 1)
                v.tensor_copy(X, HC).then_inc(x1_done, 1)
                with dve.Fori(0, LAYERS - 1) as l:
                    layer(b, l)
                layer(b, LAYERS - 1)
                for i in range(9):
                    second_layernorm(b, GROUPS - 1, i)

        @block.scalar
        def _(act):
            cp = nc.scalar.copy
            act.wait_ge(consts, N_CONST)
            act.wait_ge(w_turned, 1)
            cp(W3[0:F, :, :], pA[0:F, 0, 0:2 * F * LAYERS].rearrange("p (l c) -> p l c", l=LAYERS)
               ).then_inc(w_placed, 1)

            def projection(n, tiles):
                act.wait_ge(x_turned, n + 1)
                if not (isinstance(n, int) and n == 0):
                    act.wait_ge(val_full, n)
                cp(xT, pX[0:F, 0:C]).then_inc(x_sb, 1)
                act.wait_ge(proj_full, n + 1)
                if not (isinstance(n, int) and n == 0):
                    act.wait_ge(scr_out, n * 16)
                cp(parts[:, 0, :], pP[:, 0:C]).then_inc(high_done, 1)
                act.wait_ge(val_full, n + 1)
                cp(VA[:, tiles, :, 0:D], pV[0:P, 0:CT * F].rearrange("p (t h d) -> p t h d", t=CT, h=H)
                   ).then_inc(val_done, 1)

            def empty(b, k, n):
                _, kind, i, ago = plan_of(k)[n]
                c = back(k, ago)
                act.wait_ge(turned[kind], nth(b, c, kind, i))
                if kind == "mask":
                    t, j = i // NJ, i % NJ
                    cp(MT[:, slot(c, 2), BPP * j:BPP * j + BPP, P * t:P * t + P], misc16[0:P, :, 0:P]
                       ).then_inc(placed[kind], 1)
                elif kind == "shift":
                    cp(FQ[KS:KX, slot(c, 2), :, P * i:P * i + P], misc16[KS:KX, 0:H, 0:P]).then_inc(placed[kind], 1)
                else:
                    cp(ON[:, :, :, :], misc[0:P, :].rearrange("p (t h v) -> p t h v", t=CT, h=H)[:, :, :, 0:V]
                       ).then_inc(placed[kind], 1)

            def exp_b(b, k, u):
                act.wait_ge(sx_full, upto(b, k, UNITS, u + 1))
                if u >= 4 or not (isinstance(k, int) and k == 0):
                    act.wait_ge(pv_done, upto(b, k, T, u // 2 - 1))
                nc.scalar.activation(banks(E[0:P, u % 4, :]), bank_b(k, u)[0:P, :, 0:C], ACT.Exp, scale=0.2
                                     ).then_inc(exp_done, 1)

            def body(b, k, steps=UNITS, roots_of=None):
                plan = plan_of(k)
                n = 0
                for r in range(steps):
                    if roots_of is not None and r % GROUP_UNITS == 8 and r > GROUP_UNITS:
                        root2(roots_of, r // GROUP_UNITS - 1)
                    c, u = unit_b(k, r - LAG - 1)
                    if c is not None:
                        exp_b(b, c, u)
                    if r == LAG + 4 and exists(back(k, 2)):
                        act.wait_ge(pv_done, upto(b, back(k, 1), T, 0))
                        cp(OT[:, :], pO[:, 0:C]).then_inc(ot_done, 1)
                    while n < len(plan) and plan[n][0] <= r:
                        empty(b, k, n)
                        n += 1

            def root(sem, n, q):
                act.wait_ge(sem, n)
                nc.scalar.activation(std[:, q], var[:, q], ACT.Sqrt).then_inc(std_done, 1)

            def root2(b, g):
                root(ln2, b * (8 * GROUPS) + 8 * g + 7, slice(g * T // GROUPS, (g + 1) * T // GROUPS))

            def layer(b, l):
                n = b * LAYERS + l
                for g in range(NC + 1):
                    if g < NC:
                        act.wait_ge(ht_full, n * NC + g + 1)
                        cp(HT[0:F, C * g:C * g + C], pA[0:F, g % 2, 0:C]).then_inc(ht_done, 1)
                    if g >= 1:
                        d = g - 1
                        q = slice(CT * d, CT * d + CT)
                        w = wx[d % 4][0:P, :].rearrange("p (t c) -> p t c", t=CT)
                        act.wait_ge(wx_full, n * NC + d + 1)
                        cp(m3(q, slice(0, F)), w[:, :, F:2 * F])
                        cp(SELF[:, q, :], w[:, :, 0:F]).then_inc(self_done, 1)
                if isinstance(l, int):
                    body(b + 1, 0, roots_of=b)
                else:
                    for i in range(NC // 2):
                        projection(b * NC + l * (NC // 2) + (NC + i), bass.ds(l * (T // 2) + i * CT, CT))

            for c in range(NC):
                projection(c, slice(CT * c, CT * c + CT))
            body(0, 0)
            with act.Fori(0, B) as b:
                body(b, 1)
                with act.Fori(2, NC) as k:
                    body(b, (k, 0))
                body(b, NC)
                body(b, NC + 1, LAG + 6)
                root(ln1, b * 8 + 7, slice(0, T))
                with act.Fori(0, LAYERS - 1) as l:
                    layer(b, l)
                layer(b, LAYERS - 1)
                root2(b, GROUPS - 1)
                act.wait_ge(y_done, (b + 1) * GROUPS)
                apart(act)
                act.dma_start(out_v[b], TMP).then_inc(y_out, 16)
            act.wait_ge(y_out, (B + 1) * 16)

        @block.gpsimd
        def _(pool):
            g = nc.gpsimd
            g.memset(ident[:, :], 0.0).then_inc(ident_step, 1)
            pool.wait_ge(ident_step, 1)
            g.affine_select(out=ident[:, :], in_=ident[:, :], compare_op=ALU.not_equal, fill=1.0, base=0,
                            pattern=[[-1, 128]], channel_multiplier=1).then_inc(ident_step, 1)
            pool.wait_ge(ident_step, 2)
            g.tensor_copy(ident16[:, :], ident[:, :]).then_inc(ident_step, 1)

            def quarter(b, k):
                pool.wait_ge(fs_in, upto(b, k, 96, 96))
                if k >= 2:
                    pool.wait_ge(sx_full, upto(b, back(k, 1), UNITS, 0))
                apart(pool)
                g.tensor_scalar(FQ[0:KS, slot(k, 2), :, :], FS[:, slot(k, 3), :, :], 0.25, 1.0, ALU.mult, ALU.mult
                                ).then_inc(fq_ready, 1)

            def mask(b, k, p):
                pool.wait_ge(a_in[p % 2], upto(b, k, 8 * PIECES, (p // 2 + 1) * 16))
                if p >= 3:
                    pool.wait_ge(max_done, upto(b, k, UNITS, (p - 2) * H + 1))
                    pool.wait_ge(turned["mask"], nth(b, k, "mask", p - 3))
                elif k >= 1:
                    pool.wait_ge(max_done, upto(b, back(k, 1), UNITS, (p - 2 + PIECES) * H + 1))
                    pool.wait_ge(turned["mask"], nth(b, k, "mask", p - 3))
                apart(pool)
                g.tensor_scalar(M16[:, p % 3, :], A32[:, p % 2, :], -1.0, BIG, ALU.add, ALU.mult
                                ).then_inc(m16_ready, 1)

            def adjacency8(b, k, t):
                pool.wait_ge(placed["mask"], nth(b, k, "mask", NJ * t + NJ - 1))
                q = C * k + P * t
                apart(pool)
                g.tensor_scalar(AT[:, :, q:q + P], MT[:, slot(k, 2), :, P * t:P * t + P], ONE8 / BIG, ONE8,
                                ALU.mult, ALU.add).then_inc(at_done, 1)

            def chunk(b, k):
                for p in range(PIECES):
                    mask(b, k, p)
                    if p == 4:
                        quarter(b, k)
                    if k == 1 and 3 <= p < 3 + CT:
                        if p == 3:
                            pool.wait_ge(y_out, (b + 1) * 16)
                        adjacency8(b, 0, p - 3)
                    if k >= 1 and p % NJ == NJ - 1 and p >= 2 * NJ - 1:
                        adjacency8(b, k, p // NJ - 1)
                if k >= 1:
                    adjacency8(b, k, CT - 1)

            chunk(0, 0)
            with pool.Fori(0, B) as b:
                for k in range(1, NC):
                    chunk(b, k)
                chunk(b + 1, 0)


_INS = ["x", "adj", "L0_gnn_kernel", "L0_gnn_attention_kernel", "L0_gnn_attention_kernel_2", "L0_gnn_bias",
        "L1_gnn_Wm0", "L1_gnn_Ws0", "L1_gnn_b0", "L1_gnn_Wm1", "L1_gnn_Ws1", "L1_gnn_b1",
        "L1_gnn_Wm2", "L1_gnn_Ws2", "L1_gnn_b2"]


def kernel(**inputs):
    import concourse.bacc as bacc
    import numpy as np
    from concourse.bass_utils import run_bass_kernel_spmd

    nc = bacc.Bacc("TRN2", target_bir_lowering=False, num_devices=1, dynamic_dma_scratch_size=1024)
    arrays, args = {}, {}
    for name in _INS:
        a = np.ascontiguousarray(inputs[name])
        arrays[f"in_{name}"] = a
        args[name] = nc.dram_tensor(f"in_{name}", a.shape, mybir.dt.from_np(a.dtype), kind="ExternalInput").ap()
    out = nc.dram_tensor("out_0", (B, N, F), F32, kind="ExternalOutput").ap()
    build(nc, args["x"], args["adj"], args["L0_gnn_kernel"], args["L0_gnn_attention_kernel"],
          args["L0_gnn_attention_kernel_2"], args["L0_gnn_bias"],
          [args[f"L1_gnn_Wm{l}"] for l in range(LAYERS)], [args[f"L1_gnn_Ws{l}"] for l in range(LAYERS)],
          [args[f"L1_gnn_b{l}"] for l in range(LAYERS)], out)
    r = run_bass_kernel_spmd(nc, [arrays], core_ids=[0])
    return r.results[0]["out_0"]
```
